# Optimizing a Trainium2 kernel written in Bass

```python
import numpy as np
import jax
import jax.numpy as jnp

def _softmax(x, axis=-1):
    return jax.nn.softmax(x, axis=axis)

def _gelu(x):
    return jax.nn.gelu(x, approximate=True)

def _silu(x):
    return jax.nn.silu(x)

def _sigmoid(x):
    return jax.nn.sigmoid(x)

def _layernorm(x, axis=-1, eps=1e-05):
    m = jnp.mean(x, axis=axis, keepdims=True)
    v = jnp.var(x, axis=axis, keepdims=True)
    return (x - m) / jnp.sqrt(v + eps)

def _scatter_add(tgt, idx, src, axis=0):
    return tgt.at[idx].add(src)

def _segment_sum(src, seg, n):
    return jax.ops.segment_sum(src, seg, n)
kernel_name = 'mk_seq_postln_d1_jaxref_r8_8a5df8'

def setup_inputs(seed: int=0):
    np.random.seed(seed)
    _w = jnp.asarray

    def _L0_attn_setup():
        import jax, jax.numpy as jnp
        import numpy as np
        L, B, S, D, H, HID = (6, 4, 128, 128, 16, 512)
        HD = D // H

        def _pos_encoding(S, D):
            pos = np.arange(S)
            level = np.frexp((pos + 1).astype(np.float64))[1] - 1
            coord = (pos >> level) / 2.0 ** level
            div = np.exp(np.arange(0, D, 2, dtype=np.float64) * -(np.log(10000.0) / D))
            ang = pos[:, None].astype(np.float64) * div[None, :]
            pe = np.zeros((S, D), np.float32)
            pe[:, 0::2] = (np.sin(ang) * coord[:, None]).astype(np.float32)
            pe[:, 1::2] = (np.cos(ang) * coord[:, None]).astype(np.float32)
            return jnp.asarray(pe)

        def _sierpinski_mask(S):
            i = np.arange(S)
            return jnp.asarray((np.bitwise_and(i[:, None], i[None, :]) == 0).astype(np.float32))

        def _ln(h, g, b, eps=1e-05):
            m = h.mean(-1, keepdims=True)
            v = h.var(-1, keepdims=True)
            return (h - m) * jax.lax.rsqrt(v + eps) * g + b
        key = jax.random.key(seed)
        ks = iter(jax.random.split(key, 16))
        w = lambda k, shape: 0.02 * jax.random.normal(k, shape, jnp.float32)
        return {'x': jax.random.normal(next(ks), (B, S, D), jnp.float32), 'Wq': w(next(ks), (L, D, D)), 'bq': jnp.zeros((L, D), jnp.float32), 'Wk': w(next(ks), (L, D, D)), 'bk': jnp.zeros((L, D), jnp.float32), 'Wv': w(next(ks), (L, D, D)), 'bv': jnp.zeros((L, D), jnp.float32), 'Wo': w(next(ks), (L, D, D)), 'bo': jnp.zeros((L, D), jnp.float32), 'W1': w(next(ks), (L, D, HID)), 'b1': jnp.zeros((L, HID), jnp.float32), 'W2': w(next(ks), (L, HID, D)), 'b2': jnp.zeros((L, D), jnp.float32), 'ln1_g': jnp.ones((L, D), jnp.float32), 'ln1_b': jnp.zeros((L, D), jnp.float32), 'ln2_g': jnp.ones((L, D), jnp.float32), 'ln2_b': jnp.zeros((L, D), jnp.float32), 'lnf_g': jnp.ones((D,), jnp.float32), 'lnf_b': jnp.zeros((D,), jnp.float32)}
    _L0_attn_in = _L0_attn_setup()

    def _L0_ffn_setup():
        import jax, jax.numpy as jnp
        import numpy as np
        H = 16
        EPS = 1e-05

        def layernorm(x, g, b):
            m = jnp.mean(x, axis=-1, keepdims=True)
            v = jnp.mean((x - m) ** 2, axis=-1, keepdims=True)
            return (x - m) * jax.lax.rsqrt(v + EPS) * g + b
        key = jax.random.key(seed)
        B, S, D, E = (4, 256, 128, 8)
        ks = jax.random.split(key, 16)
        s = 0.02
        inp = {'x': jax.random.normal(ks[0], (B, S, D), jnp.float32), 'Wq': jax.random.normal(ks[1], (D, D), jnp.float32) * s, 'bq': jnp.zeros((D,), jnp.float32), 'Wk': jax.random.normal(ks[2], (D, D), jnp.float32) * s, 'bk': jnp.zeros((D,), jnp.float32), 'Wv': jax.random.normal(ks[3], (D, D), jnp.float32) * s, 'bv': jnp.zeros((D,), jnp.float32), 'Wo': jax.random.normal(ks[4], (D, D), jnp.float32) * s, 'bo': jnp.zeros((D,), jnp.float32), 'g1': jnp.ones((D,), jnp.float32), 'be1': jnp.zeros((D,), jnp.float32), 'g2': jnp.ones((D,), jnp.float32), 'be2': jnp.zeros((D,), jnp.float32), 'Wg': jax.random.normal(ks[5], (D, E), jnp.float32) * s, 'bg': jnp.zeros((E,), jnp.float32), 'We': jax.random.normal(ks[6], (E, D, D), jnp.float32) * s, 'bexp': jnp.zeros((E, D), jnp.float32)}
        return inp
    _L0_ffn_in = _L0_ffn_setup()
    _d = {'L0_attn_x': _L0_attn_in['x'], 'L0_attn_Wq': _L0_attn_in['Wq'], 'L0_attn_bq': _L0_attn_in['bq'], 'L0_attn_Wk': _L0_attn_in['Wk'], 'L0_attn_bk': _L0_attn_in['bk'], 'L0_attn_Wv': _L0_attn_in['Wv'], 'L0_attn_bv': _L0_attn_in['bv'], 'L0_attn_Wo': _L0_attn_in['Wo'], 'L0_attn_bo': _L0_attn_in['bo'], 'L0_attn_W1': _L0_attn_in['W1'], 'L0_attn_b1': _L0_attn_in['b1'], 'L0_attn_W2': _L0_attn_in['W2'], 'L0_attn_b2': _L0_attn_in['b2'], 'L0_attn_ln1_g': _L0_attn_in['ln1_g'], 'L0_attn_ln1_b': _L0_attn_in['ln1_b'], 'L0_attn_ln2_g': _L0_attn_in['ln2_g'], 'L0_attn_ln2_b': _L0_attn_in['ln2_b'], 'L0_attn_lnf_g': _L0_attn_in['lnf_g'], 'L0_attn_lnf_b': _L0_attn_in['lnf_b'], 'L0_ffn_Wq': _L0_ffn_in['Wq'], 'L0_ffn_bq': _L0_ffn_in['bq'], 'L0_ffn_Wk': _L0_ffn_in['Wk'], 'L0_ffn_bk': _L0_ffn_in['bk'], 'L0_ffn_Wv': _L0_ffn_in['Wv'], 'L0_ffn_bv': _L0_ffn_in['bv'], 'L0_ffn_Wo': _L0_ffn_in['Wo'], 'L0_ffn_bo': _L0_ffn_in['bo'], 'L0_ffn_g1': _L0_ffn_in['g1'], 'L0_ffn_be1': _L0_ffn_in['be1'], 'L0_ffn_g2': _L0_ffn_in['g2'], 'L0_ffn_be2': _L0_ffn_in['be2'], 'L0_ffn_Wg': _L0_ffn_in['Wg'], 'L0_ffn_bg': _L0_ffn_in['bg'], 'L0_ffn_We': _L0_ffn_in['We'], 'L0_ffn_bexp': _L0_ffn_in['bexp']}
    _x0 = _d['L0_attn_x']
    _d['L0_attn_x'] = jax.random.normal(jax.random.fold_in(jax.random.key(seed), 1), (4, 512, 128), dtype=_x0.dtype)
    del _x0
    return _d

def reference(L0_attn_x, L0_attn_Wq, L0_attn_bq, L0_attn_Wk, L0_attn_bk, L0_attn_Wv, L0_attn_bv, L0_attn_Wo, L0_attn_bo, L0_attn_W1, L0_attn_b1, L0_attn_W2, L0_attn_b2, L0_attn_ln1_g, L0_attn_ln1_b, L0_attn_ln2_g, L0_attn_ln2_b, L0_attn_lnf_g, L0_attn_lnf_b, L0_ffn_Wq, L0_ffn_bq, L0_ffn_Wk, L0_ffn_bk, L0_ffn_Wv, L0_ffn_bv, L0_ffn_Wo, L0_ffn_bo, L0_ffn_g1, L0_ffn_be1, L0_ffn_g2, L0_ffn_be2, L0_ffn_Wg, L0_ffn_bg, L0_ffn_We, L0_ffn_bexp):

    def _L0_attn_ref(x, Wq, bq, Wk, bk, Wv, bv, Wo, bo, W1, b1, W2, b2, ln1_g, ln1_b, ln2_g, ln2_b, lnf_g, lnf_b):
        import jax, jax.numpy as jnp
        import numpy as np
        L, B, S, D, H, HID = (6, 4, 128, 128, 16, 512)
        HD = D // H

        def _pos_encoding(S, D):
            pos = np.arange(S)
            level = np.frexp((pos + 1).astype(np.float64))[1] - 1
            coord = (pos >> level) / 2.0 ** level
            div = np.exp(np.arange(0, D, 2, dtype=np.float64) * -(np.log(10000.0) / D))
            ang = pos[:, None].astype(np.float64) * div[None, :]
            pe = np.zeros((S, D), np.float32)
            pe[:, 0::2] = (np.sin(ang) * coord[:, None]).astype(np.float32)
            pe[:, 1::2] = (np.cos(ang) * coord[:, None]).astype(np.float32)
            return jnp.asarray(pe)

        def _sierpinski_mask(S):
            i = np.arange(S)
            return jnp.asarray((np.bitwise_and(i[:, None], i[None, :]) == 0).astype(np.float32))

        def _ln(h, g, b, eps=1e-05):
            m = h.mean(-1, keepdims=True)
            v = h.var(-1, keepdims=True)
            return (h - m) * jax.lax.rsqrt(v + eps) * g + b
        Bx, Sx, Dx = x.shape
        smask = _sierpinski_mask(Sx)
        h = x + _pos_encoding(Sx, Dx)
        scale = 1.0 / jnp.sqrt(jnp.float32(HD))

        def layer(h, p):
            wq, bq_, wk, bk_, wv, bv_, wo, bo_, w1, b1_, w2, b2_, g1, be1, g2, be2 = p
            q = (h @ wq + bq_).reshape(Bx, Sx, H, HD).transpose(0, 2, 1, 3)
            k = (h @ wk + bk_).reshape(Bx, Sx, H, HD).transpose(0, 2, 1, 3)
            v = (h @ wv + bv_).reshape(Bx, Sx, H, HD).transpose(0, 2, 1, 3)
            scores = jnp.einsum('bhqd,bhkd->bhqk', q, k) * scale
            scores = scores * smask
            a = jax.nn.softmax(scores, axis=-1)
            att = jnp.einsum('bhqk,bhkd->bhqd', a, v)
            att = att.transpose(0, 2, 1, 3).reshape(Bx, Sx, Dx) @ wo + bo_
            h = _ln(h + att, g1, be1)
            ff = jax.nn.gelu(h @ w1 + b1_, approximate=False) @ w2 + b2_
            h = _ln(h + ff, g2, be2)
            return (h, None)
        params = (Wq, bq, Wk, bk, Wv, bv, Wo, bo, W1, b1, W2, b2, ln1_g, ln1_b, ln2_g, ln2_b)
        h, _ = jax.lax.scan(layer, h, params)
        return _ln(h, lnf_g, lnf_b)

    def _L0_ffn_ref(x, Wq, bq, Wk, bk, Wv, bv, Wo, bo, g1, be1, g2, be2, Wg, bg, We, bexp):
        import jax, jax.numpy as jnp
        import numpy as np
        H = 16
        EPS = 1e-05

        def layernorm(x, g, b):
            m = jnp.mean(x, axis=-1, keepdims=True)
            v = jnp.mean((x - m) ** 2, axis=-1, keepdims=True)
            return (x - m) * jax.lax.rsqrt(v + EPS) * g + b
        B, S, D = x.shape
        Dh = D // H
        TOP_K = 2
        q = (x @ Wq + bq).reshape(B, S, H, Dh)
        k = (x @ Wk + bk).reshape(B, S, H, Dh)
        v = (x @ Wv + bv).reshape(B, S, H, Dh)
        scores = jnp.einsum('bqhd,bkhd->bhqk', q, k) / jnp.sqrt(jnp.float32(Dh))
        attn = jax.nn.softmax(scores, axis=-1)
        ctx = jnp.einsum('bhqk,bkhd->bqhd', attn, v).reshape(B, S, D)
        attn_out = ctx @ Wo + bo
        x = x + layernorm(attn_out, g1, be1)
        gate_probs = jax.nn.softmax(x @ Wg + bg, axis=-1)
        top_vals, top_idx = jax.lax.top_k(gate_probs, TOP_K)
        all_out = jnp.einsum('bsd,edf->bsef', x, We) + bexp
        picked = jnp.take_along_axis(all_out, top_idx[..., None], axis=2)
        moe_out = jnp.sum(top_vals[..., None] * picked, axis=2)
        return x + layernorm(moe_out, g2, be2)
    x = L0_attn_x
    x = _layernorm(x + _L0_attn_ref(x, L0_attn_Wq, L0_attn_bq, L0_attn_Wk, L0_attn_bk, L0_attn_Wv, L0_attn_bv, L0_attn_Wo, L0_attn_bo, L0_attn_W1, L0_attn_b1, L0_attn_W2, L0_attn_b2, L0_attn_ln1_g, L0_attn_ln1_b, L0_attn_ln2_g, L0_attn_ln2_b, L0_attn_lnf_g, L0_attn_lnf_b), axis=-1)
    x = _layernorm(x + _L0_ffn_ref(x, L0_ffn_Wq, L0_ffn_bq, L0_ffn_Wk, L0_ffn_bk, L0_ffn_Wv, L0_ffn_bv, L0_ffn_Wo, L0_ffn_bo, L0_ffn_g1, L0_ffn_be1, L0_ffn_g2, L0_ffn_be2, L0_ffn_Wg, L0_ffn_bg, L0_ffn_We, L0_ffn_bexp), axis=-1)
    return x

_drawn_inputs = setup_inputs


def setup_inputs(seed=0):
    import zlib

    import numpy as np

    out = dict(_drawn_inputs(seed))
    spreads = {'L0_attn_bq': (0.0, 0.8),
     'L0_attn_bk': (0.0, 2.0),
     'L0_attn_bv': (0.0, 0.1),
     'L0_attn_bo': (0.0, 0.1),
     'L0_attn_b1': (0.0, 0.1),
     'L0_attn_b2': (0.0, 0.1),
     'L0_attn_ln1_g': (1.0, 0.2),
     'L0_attn_ln1_b': (0.0, 0.1),
     'L0_attn_ln2_g': (1.0, 0.2),
     'L0_attn_ln2_b': (0.0, 0.1),
     'L0_attn_lnf_g': (1.0, 0.2),
     'L0_attn_lnf_b': (0.0, 0.1),
     'L0_ffn_bq': (0.0, 0.496),
     'L0_ffn_bk': (0.0, 2.0),
     'L0_ffn_bv': (0.0, 0.1),
     'L0_ffn_bo': (0.0, 0.1),
     'L0_ffn_g1': (1.0, 0.2),
     'L0_ffn_be1': (0.0, 0.1),
     'L0_ffn_g2': (1.0, 0.2),
     'L0_ffn_be2': (0.0, 0.1),
     'L0_ffn_bg': (0.0, 0.1),
     'L0_ffn_bexp': (0.0, 0.1)}
    factors = {'L0_attn_Wq': 8.0, 'L0_attn_Wk': 7.194, 'L0_ffn_Wq': 2.93, 'L0_ffn_Wk': 3.074}
    for name, (base, spread) in spreads.items():
        noise = np.random.default_rng([zlib.crc32(name.encode()), seed]).standard_normal(out[name].shape)
        drawn = base * np.exp(spread * noise) if base else spread * noise
        out[name] = jnp.asarray(drawn.astype(out[name].dtype))
    for name, factor in factors.items():
        out[name] = (out[name] * factor).astype(out[name].dtype)
    return out
```

```python
import numpy as np
from contextlib import ExitStack

import concourse.bass as bass
from concourse import mybir

F32 = mybir.dt.float32
BF16 = mybir.dt.bfloat16
I32 = mybir.dt.int32
ALU = mybir.AluOpType
ACT = mybir.ActivationFunctionType
AX = mybir.AxisListType

P = 128
NB, S, D = 4, 512, 128
H, HD = 16, 8
L, HID = 6, 512
NE = 8
QT = S // P
HALF = H // 2
SCALE = float(np.float32(1.0) / np.sqrt(np.float32(HD)))
EPS = 1e-5
BIG = float(2.0 ** 100)
NMASKED = NB * L
NITEMS = NMASKED + NB
STEPS = 36
DVE_STEPS, POOL_STEPS = 8, 4 * 12
CONSTS = 8
RATES_SP = (4, 8, 64, 128, 144, 192, 384)
RATES_PE = (4, 8, 16, 32, 64, 144, 160, 192)
RATES_ACT = (4, 8, 16, 64, 144, 384)
RATES_DVE = (4, 8, 64, 128, 144)
RATES_POOL = (4, 8, 16, 48, 64, 160)
UM, UF = 36, 64
PARTS_Q = ((0, 3), (1, 2), (2, 1))
PARTS_K = ((0, 3), (0, 2), (0, 1))
ALLOWED = [[0, 1, 2, 3], [0, 2], [0, 1], [0]]


class Lin:

    def __init__(self, c, k):
        self.c, self.k = c, k

    def __add__(self, n):
        return Lin(self.c, self.k + n)

    __radd__ = __add__

    def __sub__(self, n):
        return Lin(self.c, self.k - n)

    def __mul__(self, n):
        return Lin(self.c * n, self.k * n)

    __rmul__ = __mul__


class Queue:

    def __init__(self, eng, rates, passed=None):
        self.eng, self.rates, self.passed = eng, rates, passed
        self.value = eng.alloc_register("wait_value")
        self.multiple = {c: eng.alloc_register(f"times_{c}") for c in rates}
        self.i = None

    def layers(self, n):
        with self.eng.Fori(0, n) as i:
            self.i = i
            for c in self.rates:
                self.eng.reg_mul(self.multiple[c], self.eng.to_reg(i), c)
            yield
        self.i = None

    def wait_ge(self, sem, value):
        if isinstance(value, Lin):
            if value.k == 0:
                value = self.multiple[value.c]
            else:
                self.eng.reg_add(self.value, self.multiple[value.c], value.k)
                value = self.value
            self.eng.wait_ge(sem, value)
            if self.passed is not None:
                self.eng.sem_inc(self.passed, 1)
            return
        self.eng.wait_ge(sem, value)

    def dma_start(self, out, in_):
        return self.eng.dma_start(out, in_)


class Item:

    def __init__(self, t, b, l, full):
        self.t, self.b, self.l, self.full = t, b, l, full
        self.par = b % 2
        self.last = False

    def units(self):
        return UF if self.full else UM

    def ubase(self):
        return NMASKED * UM + (self.t - NMASKED) * UF if self.full else self.t * UM

    def pbase(self):
        return NMASKED * 4 + (self.t - NMASKED) * 16 if self.full else self.t * 4


def item_at(s, k, reg=None):
    j = s + k
    if reg is None:
        if not 0 <= j < NITEMS:
            return None
        it = Item(j, j % NB, j // NB, j >= NMASKED)
        it.last = NMASKED - NB <= j < NMASKED
        return it
    return Item(Lin(NB, j), j % NB, Lin(1, j // NB), False)


class Slot:
    def __init__(self, s, reg=None):
        self.s, self.reg = s, reg
        self.A, self.B, self.C, self.Dn = (item_at(s, k, reg) for k in (2, 1, 0, -1))
        self.V = self.B

    def before(self):
        return Slot(self.s - 1, self.reg)


def slots(eng):
    for s in (-2, -1, 0):
        yield Slot(s)
    for _ in eng.layers(L - 1):
        for s in range(1, 1 + NB):
            yield Slot(s, True)
    for s in range(1 + NB * (L - 1), NITEMS + 1):
        yield Slot(s)


class Chain:

    def __init__(self, eng, sem, per_loop):
        self.eng, self.sem, self.per = eng, sem, per_loop
        self.n, self.start, self.reg = 0, None, None

    def enter(self, slot):
        if slot.reg is not None and self.reg is None:
            self.start, self.reg = self.n, slot.reg
        if slot.reg is None and self.reg is not None:
            assert self.n - self.start == self.per, (self.n - self.start, self.per)
            self.n += self.per * (L - 2)
            self.reg = None

    def inc(self, ins):
        ins.then_inc(self.sem, 1)
        self.n += 1

    def wait(self):
        self.eng.wait_ge(self.sem, self.n if self.reg is None else Lin(self.per, self.n))

    def link(self, ins):
        self.inc(ins)
        self.wait()


def unit_blocks(full, i):
    if full:
        return i // 4, [i % 4], ALLOWED[0]
    if i < 4:
        return 0, [i], ALLOWED[0]
    if i < 8:
        return (i - 2) // 2, [2 * (i % 2), 2 * (i % 2) + 1], ALLOWED[(i - 2) // 2]
    return 3, [0, 1, 2, 3], ALLOWED[3]


def layer(q, l):
    return q.i + l.k if isinstance(l, Lin) else l


def head_of(g, c):
    return HALF * (g // 2) + 2 * c + g % 2


def pick(ap, blocks):
    v = ap.rearrange("p (a n) -> p a n", n=P)
    if blocks == [0, 2]:
        return v[:, 0:3:2, :]
    return v[:, 0:len(blocks), :]


def build(nc, d, out):
    with ExitStack() as ctx:
        def sb(name, shape, dt=F32):
            return ctx.enter_context(nc.sbuf_tensor(name, shape, dt))

        def pb(name, shape, dt=F32):
            return ctx.enter_context(nc.psum_tensor(name, shape, dt))

        sems = {}

        def sem(name):
            sems[name] = ctx.enter_context(nc.semaphore(name))
            return sems[name]

        Qop = sb("Qop", [P, 2, H, S], BF16)
        Kop = sb("Kop", [P, 2, H, S], BF16)
        XS = sb("XS", [P, 2, 3, S], BF16)
        R1 = sb("R1", [P, 2, S])
        Vp = sb("Vp", [P, 2, QT, H, 32])
        PT = sb("PT", [P, 18, S])
        AU = sb("AU", [P, 2, S])
        NOTM = sb("NOTM", [P, QT, S])
        NMQ = sb("NMQ", [P, S])
        NFLOOR = sb("NFLOOR", [P, QT, HALF])
        IDF = sb("IDF", [P, P])
        IDB = sb("IDB", [P, P], BF16)
        SEL = sb("SEL", [P, 4, P])
        MX = sb("MX", [P, 2, QT, HALF])
        NM = sb("NM", [P, 2, QT, HALF])
        MR = sb("MR", [P, 2, QT, HALF])
        SPL = sb("SPL", [P, 2, QT, 3, HALF], BF16)
        MROW = sb("MROW", [3 * HALF, 2, S], BF16)
        EXM = sb("EXM", [P, QT, H])
        ER = sb("ER", [H, S])
        EM = sb("EM", [P, S])
        NUM = sb("NUM", [P, S])
        DN = sb("DN", [P, S])
        DEN = sb("DEN", [P, S])
        ATT = sb("ATT", [P, S])
        Hh = sb("Hh", [P, NB, QT, D])
        HT = sb("HT", [P, NB, S])
        HB = sb("HB", [P, QT, D])
        VC = sb("VC", [P, QT, D])
        X = sb("X", [P, QT, D])
        XN = sb("XN", [P, QT, D])
        H1 = sb("H1", [P, QT, D])
        H1T = sb("H1T", [P, S])
        HIDT = sb("HIDT", [P, QT, S])
        XR = sb("XR", [P, QT, D])
        BS = sb("BS", [P, QT, 6])
        MV = sb("MV", [P, QT, 2])
        VE = sb("VE", [P, QT])
        RS = sb("RS", [P, QT])
        NMEAN = sb("NMEAN", [P, QT])
        MHALF = sb("MHALF", [P, QT])
        Wq, Wk, Wv, Wo = (sb(n, [P, D]) for n in ("Wq", "Wk", "Wv", "Wo"))
        bqk = sb("bqk", [P, 2])
        BV = sb("BV", [P, D])
        W1 = sb("W1", [P, HID])
        W2 = sb("W2", [P, HID // P, D])
        b1 = sb("b1", [P, HID // P])
        BO, G1, BE1, B2, G2, BE2, GF, BF = (sb(n, [P, D]) for n in
                                            ("BO", "G1", "BE1", "B2", "G2", "BE2", "GF", "BF"))
        WG = sb("WG", [P, NE])
        BG = sb("BG", [P, NE])
        TRI = sb("TRI", [P, NE, NE])
        LG = sb("LG", [P, QT, NE])
        LM = sb("LM", [P, QT])
        PR = sb("PR", [P, QT, NE])
        WT = sb("WT", [P, QT, NE])
        WE = HIDT[:, 0:2, :].rearrange("p a n -> p (a n)")
        BEXP = HIDT[:, 2:4, :].rearrange("p a n -> p (a n)")
        YE = NOTM[:, 0, :]
        GT, EQ = (NOTM[:, k, 0:QT * NE * NE].rearrange("p (q e j) -> p q e j", q=QT, e=NE) for k in (1, 2))

        pS = pb("pS", [P, 2, S])
        pT = pb("pT", [P, 2, S])
        pV = pb("pV", [P, 2, S])
        pD = pb("pD", [P, 2, S])

        Qs = nc.dram_tensor("Qs", (H, HD, 6, S), BF16)[:]
        Ks = nc.dram_tensor("Ks", (H, HD, 6, S), BF16)[:]
        Ms = nc.dram_tensor("Ms", (2, 3, HALF, S), BF16)[:]
        Es = nc.dram_tensor("Es", (H, HD, S), F32)[:]

        consts_in = sem("consts_in")
        pos_in = sem("pos_in")
        x_in = sem("x_in")
        posin = sem("posin")
        ht0_filled = sem("ht0_filled")
        ht0_copied = sem("ht0_copied")
        setup_pool = sem("setup_pool")
        setup_dve = sem("setup_dve")
        opconst = sem("opconst")
        wa_in = sem("wa_in")
        wv_in = sem("wv_in")
        wd_in = sem("wd_in")
        we_in = sem("we_in")
        qk_filled = sem("qk_filled")
        hi_done = sem("hi_done")
        r1_done = sem("r1_done")
        parts_done = sem("parts_done")
        parts_out = sem("parts_out")
        placed = [sem("placed0"), sem("placed1")]
        s_filled = sem("s_filled")
        s_used = sem("s_used")
        nm_done = sem("nm_done")
        mparts_done = sem("mparts_done")
        m_filled = sem("m_filled")
        m_copied = sem("m_copied")
        m_out = sem("m_out")
        m_placed = [sem("m_placed0"), sem("m_placed1")]
        exm_done = sem("exm_done")
        e_filled = sem("e_filled")
        e_copied = sem("e_copied")
        e_out = sem("e_out")
        em_in = sem("em_in")
        tw_done = sem("tw_done")
        v_filled = sem("v_filled")
        v_done = sem("v_done")
        vp_done = sem("vp_done")
        t_filled = sem("t_filled")
        t_used = sem("t_used")
        pv_done = sem("pv_done")
        au_copied = sem("au_copied")
        wp_filled = sem("wp_filled")
        num_filled = sem("num_filled")
        den_filled = sem("den_filled")
        dn_done = sem("dn_done")
        num_done = sem("num_done")
        den_done = sem("den_done")
        rec_done = sem("rec_done")
        att_done = sem("att_done")
        hb_done = sem("hb_done")
        y_filled = sem("y_filled")
        y_used = sem("y_used")
        ln_st = sem("ln_st")
        ln_rs = sem("ln_rs")
        ln_xn = sem("ln_xn")
        h1_done = sem("h1_done")
        h1b_done = sem("h1b_done")
        h1t_filled = sem("h1t_filled")
        h1t_copied = sem("h1t_copied")
        hid_filled = sem("hid_filled")
        gelu_done = sem("gelu_done")
        y2_filled = sem("y2_filled")
        y2_used = sem("y2_used")
        h2_done = sem("h2_done")
        x2_done = sem("x2_done")
        lnf_done = sem("lnf_done")
        xr_in = sem("xr_in")
        ht_filled = sem("ht_filled")
        ht_copied = sem("ht_copied")
        gate_filled = sem("gate_filled")
        lg_done = sem("lg_done")
        pe_done = sem("pe_done")
        ex_filled = sem("ex_filled")
        ex_used = sem("ex_used")
        moe_done = sem("moe_done")
        z_done = sem("z_done")
        out_ready = sem("out_ready")
        out_done = sem("out_done")
        sp_passed, pool_passed, dve_passed = sem("sp_passed"), sem("pool_passed"), sem("dve_passed")
        dve_step = sem("dve_step")
        pool_step = sem("pool_step")

        def ln_no(it, k):
            if it.full:
                return 2 * (NMASKED - NB) + 4 * NB + 3 * (it.t - NMASKED) + k
            if it.last:
                return 2 * (NMASKED - NB) + 4 * (it.t - (NMASKED - NB)) + k
            return it.t * 2 + k

        def xn_no(it, k):
            if it.full:
                return 2 * (NMASKED - NB) + 3 * NB + 2 * (it.t - NMASKED) + k
            if it.last:
                return 2 * (NMASKED - NB) + 3 * (it.t - (NMASKED - NB)) + k
            return it.t * 2 + k

        def bank_order(sl):
            A, B, C, V, Z = sl.A, sl.B, sl.C, sl.V, sl.Dn
            masked = Z is not None and not Z.full
            full = Z is not None and Z.full
            b0 = [
                ("M1", C is not None, m_copied, C and C.t * 2 + 2),
                ("DEN", Z is not None, den_done, Z and Z.t + 1),
                ("K", A is not None, r1_done, A and A.t * 2 + 2),
                ("WP", C is not None and not C.full, tw_done, C and C.t + 1),
                ("V", V is not None, v_done, V and V.t + 1),
                ("W1_0", masked, gelu_done, Z and Z.t * 4 + 1),
                ("W1_2", masked, gelu_done, Z and Z.t * 4 + 3),
                ("GATE", full, lg_done, Z and full and Z.t - NMASKED + 1),
            ] + [(f"X{i}", full, ex_used, full and (Z.t - NMASKED) * 8 + i + 1) for i in (0, 2, 4, 6)] + [
                ("M0", B is not None, m_copied, B and B.t * 2 + 1),
                ("T2", masked, ht_copied, Z and Z.t + 1),
            ]
            b1_ = [
                ("E", C is not None and not C.full, e_copied, C and C.t + 1),
                ("NUM", Z is not None, num_done, Z and Z.t + 1),
                ("Q", A is not None, r1_done, A and A.t * 2 + 1),
                ("WO", Z is not None, y_used, Z and Z.t + 1),
                ("T1", Z is not None, h1t_copied, Z and Z.t + 1),
                ("W1_1", masked, gelu_done, Z and Z.t * 4 + 2),
                ("W1_3", masked, gelu_done, Z and Z.t * 4 + 4),
            ] + [(f"X{i}", full, ex_used, full and (Z.t - NMASKED) * 8 + i + 1) for i in (1, 3, 5, 7)] + [
                ("W2", masked, y2_used, Z and Z.t + 1),
            ]
            return b0, b1_

        def bank_for(pe, sl, name):
            for bank in (0, 1):
                order = bank_order(sl)[bank]
                names = [o[0] for o in order]
                if name not in names:
                    continue
                k = names.index(name)
                look = sl
                for _ in range(4):
                    for o in reversed(order[:k]):
                        if o[1]:
                            pe.wait_ge(o[2], o[3])
                            return pD[:, bank, :]
                    if look.s <= -2:
                        return pD[:, bank, :]
                    look = look.before()
                    order = bank_order(look)[bank]
                    k = len(order)
                return pD[:, bank, :]

        def step_units(it, step):
            n = it.units()
            return range((step * n + STEPS - 1) // STEPS, ((step + 1) * n + STEPS - 1) // STEPS)

        block = ctx.enter_context(nc.Block())

        @block.sync
        def _(sp_engine):
            sp = Queue(sp_engine, RATES_SP, sp_passed)
            def load_a(l, names=("L0_attn_Wq", "L0_attn_Wk", "L0_attn_bq", "L0_attn_bk")):
                wq, wk, bq, bk = ((d[n][l] if l is not None else d[n]) for n in names)
                sp.dma_start(Wq[:], wq).then_inc(wa_in, 16)
                sp.dma_start(Wk[:], wk).then_inc(wa_in, 16)
                sp.dma_start(bqk[:, 0:1], bq.rearrange("(p o) -> p o", o=1)).then_inc(wa_in, 16)
                sp.dma_start(bqk[:, 1:2], bk.rearrange("(p o) -> p o", o=1)).then_inc(wa_in, 16)

            def bcast(dst, row, s):
                sp.dma_start(dst, row.rearrange("(o n) -> o n", o=1).to_broadcast([P, D])).then_inc(s, 16)

            def load_v(l, pre="L0_attn_"):
                w, b = ((d[pre + n][l] if l is not None else d[pre + n]) for n in ("Wv", "bv"))
                sp.dma_start(Wv[:], w).then_inc(wv_in, 16)
                bcast(BV[:], b, wv_in)

            def load_d(l):
                sp.dma_start(Wo[:], d["L0_attn_Wo"][l]).then_inc(wd_in, 16)
                sp.dma_start(W1[:], d["L0_attn_W1"][l]).then_inc(wd_in, 16)
                sp.dma_start(W2[:], d["L0_attn_W2"][l].rearrange("(p j) n -> p j n", p=P)).then_inc(wd_in, 16)
                sp.dma_start(b1[:], d["L0_attn_b1"][l].rearrange("(p j) -> p j", p=P)).then_inc(wd_in, 16)
                for t, n in ((BO, "bo"), (G1, "ln1_g"), (BE1, "ln1_b"), (B2, "b2"), (G2, "ln2_g"), (BE2, "ln2_b")):
                    bcast(t[:], d["L0_attn_" + n][l], wd_in)

            def load_experts():
                sp.dma_start(Wo[:], d["L0_ffn_Wo"]).then_inc(wd_in, 16)
                for t, n in ((BO, "bo"), (G1, "g1"), (BE1, "be1"), (G2, "g2"), (BE2, "be2")):
                    bcast(t[:], d["L0_ffn_" + n], wd_in)
                sp.dma_start(WG[:], d["L0_ffn_Wg"]).then_inc(wd_in, 16)
                sp.dma_start(BG[:], d["L0_ffn_bg"].rearrange("(o n) -> o n", o=1).to_broadcast([P, NE])).then_inc(wd_in, 16)
                sp.dma_start(WE.rearrange("p (e n) -> p e n", e=NE),
                             d["L0_ffn_We"].rearrange("e p n -> p e n")).then_inc(wd_in, 16)
                sp.dma_start(BEXP, d["L0_ffn_bexp"].rearrange("e n -> (e n)").rearrange("(o n) -> o n", o=1)
                             .to_broadcast([P, NE * D])).then_inc(wd_in, 16)

            def store_parts(it):
                for x, dst, parts in ((0, Qs, PARTS_Q), (1, Ks, PARTS_K)):
                    sp.wait_ge(parts_done, it.t * 2 + 1 + x)
                    r = 0
                    for p0, n in parts:
                        src = (XS[:, x, p0:p0 + 1, :].to_broadcast([P, n, S]) if x == 0
                               else XS[:, x, p0:p0 + n, :])
                        sp.dma_start(dst.rearrange("h e r n -> (h e) r n")[:, r:r + n, :], src).then_inc(parts_out, 16)
                        r += n

            def place(it, u):
                hs = slice(HALF * u, HALF * (u + 1))
                for op, src in ((Qop, Qs), (Kop, Ks)):
                    sp.dma_start(op[0:48, it.par, hs, :],
                                 src[hs].rearrange("h e r n -> (e r) h n")).then_inc(placed[u], 16)
                z0 = 48 if it.full else 57
                sp.dma_start(Qop[z0:60, it.par, hs, :],
                             d["c_zero"][0:60 - z0].rearrange("p (h n) -> p h n", h=HALF)).then_inc(placed[u], 16)

            def shift_rows(it, u):
                sp.wait_ge(m_copied, it.t * 2 + 1 + u)
                sp.dma_start(Ms[u].rearrange("p h n -> (p h) n"), MROW[:, u, :]).then_inc(m_out, 16)
                sp.wait_ge(m_out, it.t * 32 + 16 * (u + 1))
                sp.dma_start(Qop[57:60, it.par, HALF * u:HALF * (u + 1), :], Ms[u]).then_inc(m_placed[u], 16)

            for b in range(NB):
                sp.dma_start(Hh[:, b], d["L0_attn_x"][b].rearrange("(q p) n -> p q n", p=P)).then_inc(x_in, 16)
                if b == 0:
                    sp.dma_start(XR[:], d["c_pos"].rearrange("(q p) n -> p q n", p=P)).then_inc(pos_in, 16)
                    sp.dma_start(IDF[:], d["c_idf"]).then_inc(pos_in, 16)
                    load_a(0)
            sp.dma_start(IDB[:], d["c_idb"]).then_inc(consts_in, 16)
            sp.dma_start(NFLOOR[:], d["c_nfloor"].rearrange("p (q h) -> p q h", q=QT)).then_inc(consts_in, 16)
            sp.wait_ge(setup_pool, 2)
            sp.wait_ge(setup_dve, 2)
            for par in range(2):
                sp.dma_start(Kop[48:60, par], d["c_krows"].rearrange("p (o n) -> p o n", o=1)
                             .to_broadcast([12, H, S])).then_inc(opconst, 16)
                sp.dma_start(Qop[48:57, par], d["c_qrows"].rearrange("p (o n) -> p o n", o=1)
                             .to_broadcast([9, H, S])).then_inc(opconst, 16)
            load_v(0)
            sp.dma_start(NOTM[:], d["c_notm"].rearrange("(q p) n -> p q n", p=P)).then_inc(consts_in, 16)
            sp.dma_start(NMQ[:], d["c_nmq"].rearrange("(o n) -> o n", o=1).to_broadcast([P, S])).then_inc(consts_in, 16)
            sp.dma_start(SEL[:], d["c_sel"].rearrange("(k p) n -> p k n", p=P)).then_inc(consts_in, 16)
            sp.dma_start(TRI[:], d["c_tri"].rearrange("p (a b) -> p a b", a=NE)).then_inc(consts_in, 16)
            load_d(0)
            bcast(GF[:], d["L0_attn_lnf_g"], consts_in)
            bcast(BF[:], d["L0_attn_lnf_b"], consts_in)

            for sl in slots(sp):
                A, B, C, Z = sl.A, sl.B, sl.C, sl.Dn
                if B is not None:
                    if sl.s >= 1:
                        sp.wait_ge(t_filled, C.ubase())
                    sp.wait_ge(parts_out, B.t * 96 + 96)
                    place(B, 1)
                if C is not None:
                    shift_rows(C, 1)
                    if not C.full:
                        sp.wait_ge(e_copied, C.t + 1)
                        if sl.s >= 1:
                            sp.wait_ge(em_in, C.t * 16)
                        sp.dma_start(Es, ER[:, :].rearrange("h (o n) -> h o n", o=1)
                                     .to_broadcast([H, HD, S])).then_inc(e_out, 16)
                        sp.wait_ge(e_out, C.t * 16 + 16)
                        if sl.s >= 1:
                            sp.wait_ge(dn_done, C.t)
                            sp.wait_ge(tw_done, C.t)
                        sp.dma_start(EM[:], Es.rearrange("h e n -> (h e) n")).then_inc(em_in, 16)
                if A is not None:
                    if B is not None:
                        sp.wait_ge(placed[0], B.t * 48 + 48)
                        sp.wait_ge(placed[1], B.t * 48 + 48)
                    store_parts(A)
                    sp.wait_ge(parts_out, A.t * 96 + 96)
                    if C is not None:
                        sp.wait_ge(t_filled, C.ubase() + C.units() // 2)
                    else:
                        sp.wait_ge(opconst, 64)
                    place(A, 0)
                if Z is not None and Z.last:
                    if Z.b > 0:
                        sp.wait_ge(lnf_done, Z.b)
                    else:
                        sp.wait_ge(posin, NB)
                    sp.dma_start(XR[:], d["L0_attn_x"][Z.b].rearrange("(q p) n -> p q n", p=P)).then_inc(xr_in, 16)
                if B is not None:
                    shift_rows(B, 0)
                if A is not None and A.b == NB - 1 and (sl.reg is not None or A.l < L):
                    sp.wait_ge(r1_done, A.t * 2 + 2)
                    if sl.reg is None and A.l == L - 1:
                        load_a(None, ("L0_ffn_Wq", "L0_ffn_Wk", "L0_ffn_bq", "L0_ffn_bk"))
                    else:
                        load_a(layer(sp, A.l + 1))
                if B is not None and B.b == NB - 1 and (sl.reg is not None or B.l < L):
                    sp.wait_ge(v_done, B.t + 1)
                    if sl.reg is None and B.l == L - 1:
                        load_v(None, "L0_ffn_")
                    else:
                        load_v(layer(sp, B.l + 1))
                if Z is not None and Z.b == NB - 1 and not Z.full:
                    sp.wait_ge(ht_copied, Z.t + 1)
                    if Z.last:
                        load_experts()
                    else:
                        load_d(layer(sp, Z.l + 1))
                if Z is not None and Z.full:
                    sp.wait_ge(out_ready, Z.t - NMASKED + 1)
                    sp.dma_start(out[Z.b].rearrange("(q p) n -> p q n", p=P), H1[:]).then_inc(out_done, 16)
            sp.wait_ge(out_done, 16 * NB)

        @block.tensor
        def _(pe_engine):
            pe = Queue(pe_engine, RATES_PE)
            mm = nc.tensor.matmul

            def score_unit(it, k, maxima):
                n = it.ubase() + k
                g, i = divmod(k, 16 if it.full else 9)
                tile, heads, blocks = unit_blocks(it.full, i)
                u = g // 2
                if maxima:
                    if i == 0 and g % 2 == 0:
                        pe.wait_ge(placed[u], it.t * 48 + 48)
                    filled, used, bank = s_filled, s_used, pS[:, k % 2, :]
                    st, mv = Qop, Kop
                else:
                    if i == 0 and g % 2 == 0:
                        pe.wait_ge(m_placed[u], it.t * 16 + 16)
                    filled, used, bank = t_filled, t_used, pT[:, k % 2, :]
                    st, mv = Kop, Qop
                if not (isinstance(n, int) and n < 2):
                    pe.wait_ge(used, n - 1)
                w = P * len(blocks)
                for x, c in enumerate(heads):
                    h = head_of(g, c)
                    ins = mm(bank[:, x * w:(x + 1) * w], st[:, it.par, h, tile * P:(tile + 1) * P],
                             pick(mv[:, it.par, h, :], blocks), start=True, stop=True)
                ins.then_inc(filled, 1)

            def value_product(it, g, tiles):
                u, v = divmod(g, 2)
                if v == 0 and tiles[0] == 0 and not (isinstance(it.t, int) and it.t == 0):
                    pe.wait_ge(au_copied, it.t * 2 - 1 + u)
                if g == 0 and tiles[0] == 0:
                    pe.wait_ge(vp_done, it.t + 1)
                if it.full:
                    pe.wait_ge(t_used, it.ubase() + 16 * g + 4 * tiles[0] + 4)
                else:
                    pe.wait_ge(t_used, it.ubase() + 9 * g + 9)
                for kt in tiles:
                    for c in range(4):
                        h = head_of(g, c)
                        if it.full:
                            src = PT[:, 4 * kt + c, :]
                            blocks = ALLOWED[0]
                        else:
                            blocks = ALLOWED[kt]
                            w = P * len(blocks)
                            for i in range(9):
                                tile, heads, _ = unit_blocks(False, i)
                                if tile == kt and c in heads:
                                    x = heads.index(c)
                                    src = PT[:, 9 * (g % 2) + i, x * w:(x + 1) * w]
                        first = v == 0 and kt == 0
                        last = v == 1 and kt == 3
                        ins = mm(pick(pV[32 * c:32 * c + 32, u, :], blocks),
                                 Vp[:, it.par, kt, h, :], src, start=first, stop=last, skip_group_check=True,
                                 tile_position=(0, 32 * c))
                ins.then_inc(pv_done, 1)

            def transposes(bank, src, ident, rows):
                for q in range(QT):
                    ins = nc.tensor.transpose(bank[0:rows, q * P:(q + 1) * P], src(q), ident)
                return ins

            def shift_transpose(sl, it, u):
                pe.wait_ge(mparts_done, it.t * 2 + 1 + u)
                bank = bank_for(pe, sl, "M1" if u else "M0").bitcast(BF16)
                transposes(bank, lambda q: SPL[:, u, q].rearrange("p a h -> p (a h)"), IDB[:], 3 * HALF) \
                    .then_inc(m_filled, 1)

            pe.wait_ge(pos_in, 32)
            for b in range(NB):
                pe.wait_ge(posin, b + 1)
                if b >= 2:
                    pe.wait_ge(ht0_copied, b - 1)
                transposes(pD[:, b % 2, :], lambda q: Hh[:, b, q, :], IDF[:], P).then_inc(ht0_filled, 1)
            pe.wait_ge(ht0_copied, NB)
            pe.wait_ge(consts_in, CONSTS * 16)

            for sl in slots(pe):
                A, B, C, V, Z = sl.A, sl.B, sl.C, sl.V, sl.Dn
                prev_last = Z is not None
                if C is not None and C.full and C.b == 0:
                    value_product(Z, 3, range(QT))
                    prev_last = False
                for step in range(STEPS):
                    if B is not None:
                        for k in step_units(B, step):
                            score_unit(B, k, True)
                    if C is not None:
                        for k in step_units(C, step):
                            score_unit(C, k, False)
                            if C.full and k % 4 == 1 and k >= 5:
                                qd = k // 4 - 1
                                value_product(C, qd // 4, [qd % 4])
                    if step == 2 and C is not None:
                        shift_transpose(sl, C, 1)
                    if step == 4 and prev_last:
                        if Z.full:
                            value_product(Z, 3, [3])
                        else:
                            value_product(Z, 3, range(QT))
                    if step == 5 and C is not None and not C.full:
                        pe.wait_ge(exm_done, C.t + 1)
                        bank = bank_for(pe, sl, "E")
                        transposes(bank, lambda q: EXM[:, q, :], IDF[:], H).then_inc(e_filled, 1)
                    if step == 7 and Z is not None:
                        pe.wait_ge(au_copied, Z.t * 2 + 2)
                        for name, k0, s in (("NUM", 0, num_filled), ("DEN", 2, den_filled)):
                            bank = bank_for(pe, sl, name)
                            for u in range(2):
                                ins = mm(bank, SEL[:, k0 + u, :], AU[:, u, :], start=u == 0, stop=u == 1)
                            ins.then_inc(s, 1)
                    if step in (8, 10) and A is not None:
                        if step == 8:
                            pe.wait_ge(wa_in, A.l * 64 + 64)
                            if sl.s >= 2 or sl.reg is not None:
                                pe.wait_ge(ht_copied, A.t - NB + 1)
                        bank = bank_for(pe, sl, "Q" if step == 8 else "K")
                        mm(bank, (Wq if step == 8 else Wk)[:], HT[:, A.b, :], start=True, stop=True) \
                            .then_inc(qk_filled, 1)
                    if step == 13:
                        if Z is not None:
                            pe.wait_ge(att_done, Z.t + 1)
                            pe.wait_ge(wd_in, Z.l * 160 + 160)
                            bank = bank_for(pe, sl, "WO")
                            for q in range(QT):
                                ins = mm(bank[:, q * P:(q + 1) * P], ATT[:, q * P:(q + 1) * P], Wo[:],
                                         start=True, stop=True)
                            ins.then_inc(y_filled, 1)
                        if C is not None and not C.full:
                            value_product(C, 0, range(QT))
                    if step == 14 and C is not None and not C.full:
                        pe.wait_ge(v_done, C.t + 1)
                        bank = bank_for(pe, sl, "WP")
                        for kt in range(QT):
                            ins = mm(bank, VC[:, kt, :], NOTM[:, kt, :], start=kt == 0, stop=kt == QT - 1)
                        ins.then_inc(wp_filled, 1)
                    if step == 15 and V is not None:
                        pe.wait_ge(wv_in, V.l * 32 + 32)
                        bank = bank_for(pe, sl, "V")
                        for q in range(QT):
                            ins = mm(bank[:, q * P:(q + 1) * P], HT[:, V.b, q * P:(q + 1) * P], Wv[:],
                                     start=True, stop=True)
                        ins.then_inc(v_filled, 1)
                    if step == 19 and Z is not None:
                        pe.wait_ge(h1_done, Z.t + 1)
                        bank = bank_for(pe, sl, "T1")
                        transposes(bank, lambda q: H1[:, q, :], IDF[:], P).then_inc(h1t_filled, 1)
                    if step == 22:
                        if Z is not None and not Z.full:
                            pe.wait_ge(h1t_copied, Z.t + 1)
                            for j in range(HID // P):
                                bank = bank_for(pe, sl, f"W1_{j}")
                                mm(bank, W1[:, j:HID:HID // P], H1T[:], start=True, stop=True) \
                                    .then_inc(hid_filled, 1)
                        if C is not None and not C.full:
                            value_product(C, 1, range(QT))
                        if Z is not None and Z.full:
                            pe.wait_ge(h1t_copied, Z.t + 1)
                            bank = bank_for(pe, sl, "GATE")
                            for q in range(QT):
                                ins = mm(bank[:, q * NE:(q + 1) * NE], H1T[:, q * P:(q + 1) * P], WG[:],
                                         start=True, stop=True)
                            ins.then_inc(gate_filled, 1)
                            for i in range(8):
                                q, e0 = divmod(i, 2)
                                bank = bank_for(pe, sl, f"X{i}")
                                mm(bank, H1T[:, q * P:(q + 1) * P], WE[:, e0 * S:(e0 + 1) * S],
                                   start=True, stop=True).then_inc(ex_filled, 1)
                    if step == 23 and B is not None:
                        shift_transpose(sl, B, 0)
                    if step == 27 and Z is not None and not Z.full:
                        pe.wait_ge(gelu_done, Z.t * 4 + 4)
                        bank = bank_for(pe, sl, "W2")
                        for q in range(QT):
                            for j in range(HID // P):
                                ins = mm(bank[:, q * P:(q + 1) * P], HIDT[:, j, q * P:(q + 1) * P], W2[:, j, :],
                                         start=j == 0, stop=j == HID // P - 1)
                        ins.then_inc(y2_filled, 1)
                    if step == 31 and C is not None and not C.full:
                        value_product(C, 2, range(QT))
                    if step == 33 and Z is not None and not Z.full:
                        pe.wait_ge(h2_done, Z.t + 1)
                        bank = bank_for(pe, sl, "T2")
                        transposes(bank, lambda q: Hh[:, Z.b, q, :], IDF[:], P).then_inc(ht_filled, 1)

        @block.scalar
        def _(act_engine):
            act = Queue(act_engine, RATES_ACT)
            ac = nc.scalar

            def exp_unit(it, k):
                n = it.ubase() + k
                g, i = divmod(k, 16 if it.full else 9)
                act.wait_ge(t_filled, n + 1)
                if it.full:
                    qd = k // 4
                    if i % 4 == 0:
                        act.wait_ge(pv_done, it.pbase() + (qd - 3 if qd >= 4 else (0 if it.b == 0 else qd - 3)))
                    dst = PT[:, 4 * (qd % 4) + k % 4, :]
                else:
                    if i == 0 and not (isinstance(it.t, int) and it.t == 0 and g < 2):
                        act.wait_ge(pv_done, it.pbase() + g - 1)
                    dst = PT[:, 9 * (g % 2) + i, :]
                ac.activation(dst, pT[:, k % 2, :], ACT.Exp, scale=SCALE).then_inc(t_used, 1)

            def copy_au(it, u):
                act.wait_ge(pv_done, it.pbase() + (8 if it.full else 2) * (u + 1))
                if not (isinstance(it.t, int) and it.t == 0):
                    act.wait_ge(num_filled, it.t)
                    act.wait_ge(den_filled, it.t)
                ac.copy(AU[:, u, :], pV[:, u, :]).then_inc(au_copied, 1)

            for b in range(NB):
                act.wait_ge(ht0_filled, b + 1)
                ac.copy(HT[:, b, :], pD[:, b % 2, :]).then_inc(ht0_copied, 1)

            for sl in slots(act):
                A, B, C, V, Z = sl.A, sl.B, sl.C, sl.V, sl.Dn
                for step in range(STEPS):
                    if C is not None:
                        for k in step_units(C, step):
                            exp_unit(C, k)
                    if step == 3 and C is not None and not C.full:
                        act.wait_ge(nm_done, C.t * 2 + 2)
                        if sl.s >= 1:
                            act.wait_ge(e_filled, C.t)
                        for u in range(2):
                            ins = ac.activation(EXM[:, :, HALF * u:HALF * (u + 1)], NM[:, u], ACT.Exp, scale=SCALE)
                        ins.then_inc(exm_done, 1)
                    if step == 5 and Z is not None:
                        copy_au(Z, 1)
                    if step == 6 and C is not None and not C.full:
                        act.wait_ge(e_filled, C.t + 1)
                        if sl.s >= 1:
                            act.wait_ge(e_out, C.t * 16)
                        ac.copy(ER[:], pD[0:H, 1, :]).then_inc(e_copied, 1)
                    if step in (9, 11) and A is not None:
                        x = 0 if step == 9 else 1
                        act.wait_ge(qk_filled, A.t * 2 + 1 + x)
                        if sl.s >= -1:
                            act.wait_ge(parts_out, A.t * 96)
                        ac.activation(XS[:, x, 0, :], pD[:, 1 - x, :], ACT.Identity, bias=bqk[:, x:x + 1]) \
                            .then_inc(hi_done, 1)
                    if step == 20 and Z is not None:
                        act.wait_ge(h1t_filled, Z.t + 1)
                        if sl.s >= 2 or sl.reg is not None:
                            if Z.full and Z.b > 0:
                                act.wait_ge(ex_filled, 8 * Z.b)
                            else:
                                act.wait_ge(hid_filled, Z.t * 4)
                        ac.copy(H1T[:], pD[:, 1, :]).then_inc(h1t_copied, 1)
                    if step == 22 and Z is not None and not Z.full:
                        if sl.s >= 2 or sl.reg is not None:
                            act.wait_ge(y2_filled, Z.t)
                        for j in range(HID // P):
                            act.wait_ge(hid_filled, Z.t * 4 + j + 1)
                            ac.activation(HIDT[:, j, :], pD[:, j % 2, :], ACT.Gelu, bias=b1[:, j:j + 1]) \
                                .then_inc(gelu_done, 1)
                    if step == 22 and Z is not None and Z.full:
                        act.wait_ge(lg_done, Z.t - NMASKED + 1)
                        ac.activation(PR[:], LG[:], ACT.Exp).then_inc(pe_done, 1)
                    if step == 24 and C is not None:
                        if not C.full:
                            copy_au(C, 0)
                    if step == 21 and C is not None and C.full:
                        copy_au(C, 0)
                    if step == 34 and Z is not None and not Z.full:
                        act.wait_ge(ht_filled, Z.t + 1)
                        ac.copy(HT[:, Z.b, :], pD[:, 0, :]).then_inc(ht_copied, 1)

        @block.vector
        def _(dve_engine):
            dve = Queue(dve_engine, RATES_DVE)
            ve = nc.vector
            ch = Chain(dve, dve_step, DVE_STEPS)

            def max_unit(it, k):
                n = it.ubase() + k
                g, i = divmod(k, 16 if it.full else 9)
                tile, heads, blocks = unit_blocks(it.full, i)
                u, v = divmod(g, 2)
                dve.wait_ge(s_filled, n + 1)
                w = P * len(blocks)
                hs = 2 * heads[0] + v
                ve.tensor_reduce(MX[:, u, tile, hs:hs + 2 * len(heads) - 1:2],
                                 pS[:, k % 2, :].rearrange("p (h n) -> p h n", n=w),
                                 axis=AX.X, op=ALU.max).then_inc(s_used, 1)

            def neg_max(it, u):
                dve.wait_ge(s_used, it.ubase() + it.units() // 2 * (u + 1))
                if not (isinstance(it.t, int) and it.t == 0):
                    dve.wait_ge(mparts_done, it.t * 2 - 1 + u)
                    if not it.full:
                        dve.wait_ge(exm_done, it.t)
                    else:
                        dve.wait_ge(exm_done, NMASKED)
                if it.full:
                    ve.tensor_scalar(NM[:, u], MX[:, u], -1.0, None, ALU.mult).then_inc(nm_done, 1)
                else:
                    ve.scalar_tensor_tensor(out=NM[:, u], in0=MX[:, u], scalar=-1.0, in1=NFLOOR[:],
                                            op0=ALU.mult, op1=ALU.min).then_inc(nm_done, 1)

            def copy_shift(it, u):
                dve.wait_ge(m_filled, it.t * 2 + 1 + u)
                if not (isinstance(it.t, int) and it.t == 0):
                    dve.wait_ge(m_out, it.t * 32 - 16 + 16 * u)
                ve.tensor_copy(MROW[:, u, :], pD[0:3 * HALF, 0, :].bitcast(BF16)[:, 0:S]).then_inc(m_copied, 1)

            def stats(it, k):
                for q in range(QT):
                    ins = ve.bn_stats(BS[:, q, :], X[:, q, :])
                ch.link(ins)
                dve.eng.sem_inc(dve_passed, 1)
                for q in range(QT):
                    ins = ve.bn_aggr(MV[:, q, :], BS[:, q, :])
                ins.then_inc(ln_st, 1)

            def normalise(it, k):
                n = ln_no(it, k)
                dve.wait_ge(ln_rs, n + 1)
                for q in range(QT):
                    ins = ve.tensor_scalar(XN[:, q, :], X[:, q, :], NMEAN[:, q:q + 1], RS[:, q:q + 1],
                                           ALU.add, ALU.mult)
                ins.then_inc(ln_xn, 1)

            def gate(it):
                i = it.t - NMASKED
                dve.wait_ge(gate_filled, i + 1)
                ch.link(ve.tensor_tensor(LG[:], pD[:, 0, 0:QT * NE].rearrange("p (q e) -> p q e", e=NE),
                                         BG[:, :].unsqueeze(1).to_broadcast([P, QT, NE]), ALU.add))
                ch.link(ve.tensor_reduce(LM[:], LG[:], axis=AX.X, op=ALU.max))
                ve.tensor_tensor(LG[:], LG[:], LM[:, :].unsqueeze(2).to_broadcast([P, QT, NE]),
                                 ALU.subtract).then_inc(lg_done, 1)
                dve.wait_ge(pe_done, i + 1)
                ch.link(ve.tensor_reduce(LM[:], PR[:], axis=AX.X, op=ALU.add))
                ch.link(ve.reciprocal(LM[:], LM[:]))
                ch.link(ve.tensor_tensor(PR[:], PR[:], LM[:, :].unsqueeze(2).to_broadcast([P, QT, NE]), ALU.mult))
                pj = PR[:].unsqueeze(2).to_broadcast([P, QT, NE, NE])
                pe_ = PR[:].unsqueeze(3).to_broadcast([P, QT, NE, NE])
                ve.tensor_tensor(GT, pj, pe_, ALU.is_gt)
                ch.link(ve.tensor_tensor(EQ, pj, pe_, ALU.is_equal))
                ch.link(ve.tensor_tensor(EQ, EQ, TRI[:].unsqueeze(1).to_broadcast([P, QT, NE, NE]), ALU.mult))
                ch.link(ve.tensor_tensor(GT, GT, EQ, ALU.add))
                ch.link(ve.tensor_reduce(LG[:], GT, axis=AX.X, op=ALU.add))
                ch.link(ve.scalar_tensor_tensor(out=WT[:], in0=LG[:], scalar=2.0, in1=PR[:],
                                                op0=ALU.is_lt, op1=ALU.mult))

            def experts(it):
                for i in range(8):
                    q, e0 = divmod(i, 2)
                    dve.wait_ge(ex_filled, (it.t - NMASKED) * 8 + i + 1)
                    ve.tensor_tensor(YE, pD[:, i % 2, :], BEXP[:, e0 * S:(e0 + 1) * S], ALU.add).then_inc(ex_used, 1)
                    dve.wait_ge(ex_used, (it.t - NMASKED) * 8 + i + 1)
                    for e in range(4):
                        w = WT[:, q, 4 * e0 + e:4 * e0 + e + 1]
                        y = YE[:, e * P:(e + 1) * P]
                        if e0 == 0 and e == 0:
                            ch.link(ve.tensor_scalar(X[:, q, :], y, w, None, ALU.mult))
                        else:
                            ch.link(ve.scalar_tensor_tensor(out=X[:, q, :], in0=y, scalar=w, in1=X[:, q, :],
                                                            op0=ALU.mult, op1=ALU.add))

            ve.memset(Kop[:].rearrange("p a h n -> p (a h n)").bitcast(I32), 0).then_inc(setup_dve, 1)
            ve.memset(MHALF[:], -0.5).then_inc(setup_dve, 1)
            dve.wait_ge(pos_in, 32)
            for b in range(NB):
                dve.wait_ge(x_in, NB * 16)
                ve.tensor_tensor(Hh[:, b], Hh[:, b], XR[:], ALU.add).then_inc(posin, 1)
            dve.wait_ge(setup_pool, 5)
            dve.wait_ge(consts_in, CONSTS * 16)

            for sl in slots(dve):
                ch.enter(sl)
                A, B, C, V, Z = sl.A, sl.B, sl.C, sl.V, sl.Dn
                if C is not None:
                    neg_max(C, 1)
                for step in range(STEPS):
                    if B is not None:
                        for k in step_units(B, step):
                            max_unit(B, k)
                    if step == 3 and C is not None:
                        copy_shift(C, 1)
                    if step == 8 and Z is not None:
                        dve.wait_ge(num_filled, Z.t + 1)
                        if sl.s >= 2 or sl.reg is not None:
                            dve.wait_ge(att_done, Z.t)
                        if not Z.full:
                            dve.wait_ge(tw_done, Z.t + 1)
                            ve.tensor_tensor(NUM[:], pD[:, 1, :], NUM[:], ALU.add).then_inc(num_done, 1)
                            dve.wait_ge(den_filled, Z.t + 1)
                            dve.wait_ge(dn_done, Z.t + 1)
                            ve.tensor_tensor(DEN[:], pD[:, 0, :], DN[:], ALU.add).then_inc(den_done, 1)
                        else:
                            ve.tensor_copy(NUM[:], pD[:, 1, :]).then_inc(num_done, 1)
                            dve.wait_ge(den_filled, Z.t + 1)
                            ve.tensor_copy(DEN[:], pD[:, 0, :]).then_inc(den_done, 1)
                        dve.wait_ge(den_done, Z.t + 1)
                        ve.reciprocal(DEN[:], DEN[:]).then_inc(rec_done, 1)
                    if step in (9, 11) and A is not None:
                        x = 0 if step == 9 else 1
                        dve.wait_ge(hi_done, A.t * 2 + 1 + x)
                        if sl.s >= -1:
                            dve.wait_ge(parts_done, A.t * 2 - 1 + x)
                        ve.scalar_tensor_tensor(out=R1[:, x, :], in0=pD[:, 1 - x, :], scalar=bqk[:, x:x + 1],
                                                in1=XS[:, x, 0, :], op0=ALU.add, op1=ALU.subtract) \
                            .then_inc(r1_done, 1)
                    if step == 14 and Z is not None:
                        dve.wait_ge(y_filled, Z.t + 1)
                        dve.wait_ge(hb_done, Z.t + 1)
                        ve.tensor_tensor(X[:].rearrange("p q n -> p (q n)"), pD[:, 1, :],
                                         HB[:].rearrange("p q n -> p (q n)"), ALU.add).then_inc(y_used, 1)
                        dve.wait_ge(y_used, Z.t + 1)
                        stats(Z, 0)
                    if step == 14 and C is not None and not C.full:
                        dve.wait_ge(wp_filled, C.t + 1)
                        dve.wait_ge(em_in, C.t * 16 + 16)
                        if sl.s >= 1:
                            dve.wait_ge(att_done, C.t)
                        ve.tensor_tensor(NUM[:], pD[:, 0, :], EM[:], ALU.mult).then_inc(tw_done, 1)
                    if step == 16:
                        if V is not None:
                            dve.wait_ge(v_filled, V.t + 1)
                            if sl.s >= 0:
                                dve.wait_ge(vp_done, V.t)
                                if C is not None and not C.full:
                                    dve.wait_ge(wp_filled, V.t)
                            ve.tensor_tensor(VC[:], pD[:, 0, :].rearrange("p (q n) -> p q n", q=QT),
                                             BV[:, :].unsqueeze(1).to_broadcast([P, QT, D]), ALU.add) \
                                .then_inc(v_done, 1)
                    if step == 15 and Z is not None:
                        normalise(Z, 0)
                    if step == 19 and B is not None:
                        neg_max(B, 0)
                    if step == 22 and Z is not None and Z.full:
                        gate(Z)
                        experts(Z)
                        stats(Z, 1)
                    if step == 24 and B is not None:
                        copy_shift(B, 0)
                    if step == 25 and Z is not None and Z.full:
                        normalise(Z, 1)
                        dve.wait_ge(z_done, Z.t - NMASKED + 1)
                        stats(Z, 2)
                        n = ln_no(Z, 2)
                        dve.wait_ge(ln_rs, n + 1)
                        for q in range(QT):
                            ins = ve.tensor_scalar(H1[:, q, :], X[:, q, :], NMEAN[:, q:q + 1], RS[:, q:q + 1],
                                                   ALU.add, ALU.mult)
                        ins.then_inc(out_ready, 1)
                    if step == 28 and Z is not None and not Z.full:
                        dve.wait_ge(y2_filled, Z.t + 1)
                        dve.wait_ge(h1b_done, Z.t + 1)
                        ve.tensor_tensor(X[:].rearrange("p q n -> p (q n)"), pD[:, 1, :],
                                         HB[:].rearrange("p q n -> p (q n)"), ALU.add).then_inc(y2_used, 1)
                        dve.wait_ge(y2_used, Z.t + 1)
                        stats(Z, 1)
                    if step == 29 and Z is not None and not Z.full:
                        normalise(Z, 1)
                        if Z.last:
                            dve.wait_ge(x2_done, Z.b + 1)
                            stats(Z, 2)
                            normalise(Z, 2)
                            dve.wait_ge(lnf_done, Z.b + 1)
                            stats(Z, 3)
                            dve.wait_ge(ln_rs, ln_no(Z, 3) + 1)
                            for q in range(QT):
                                ins = ve.tensor_scalar(Hh[:, Z.b, q, :], X[:, q, :], NMEAN[:, q:q + 1], RS[:, q:q + 1],
                                                       ALU.add, ALU.mult)
                            ins.then_inc(h2_done, 1)
            ch.enter(Slot(NITEMS + 1))

        @block.gpsimd
        def _(pool_engine):
            pool = Queue(pool_engine, RATES_POOL, pool_passed)
            gp = nc.gpsimd
            ch = Chain(pool, pool_step, POOL_STEPS)

            def split_max(it, u):
                pool.wait_ge(nm_done, it.t * 2 + 1 + u)
                if not (isinstance(it.t, int) and it.t == 0):
                    pool.wait_ge(m_filled, it.t * 2 - 1 + u)
                ch.link(gp.tensor_copy(SPL[:, u, :, 0, :], NM[:, u]))
                ch.link(gp.tensor_tensor(MR[:, u], NM[:, u], SPL[:, u, :, 0, :], ALU.subtract))
                ch.link(gp.tensor_copy(SPL[:, u, :, 1, :], MR[:, u]))
                gp.tensor_tensor(SPL[:, u, :, 2, :], MR[:, u], SPL[:, u, :, 1, :], ALU.subtract) \
                    .then_inc(mparts_done, 1)

            def inverse_std(it, k):
                n = ln_no(it, k)
                pool.wait_ge(ln_st, n + 1)
                gp.tensor_scalar(NMEAN[:], MV[:, :, 0], -1.0, None, ALU.mult)
                ch.link(gp.tensor_scalar(VE[:], MV[:, :, 1], EPS, None, ALU.add))
                gp.tensor_tensor(RS[:], VE[:], MHALF[:], ALU.pow).then_inc(ln_rs, 1)

            def rows(t):
                return t[:].unsqueeze(1).to_broadcast([P, QT, D])

            def affine(it, k, gain, bias, dst, *more):
                pool.wait_ge(ln_xn, xn_no(it, k) + 1)
                ch.link(gp.tensor_tensor(dst, XN[:], rows(gain), ALU.mult))
                ins = gp.tensor_tensor(dst, dst, rows(bias), ALU.add)
                for m in more:
                    ch.link(ins)
                    ins = gp.tensor_tensor(dst, dst, m, ALU.add)
                return ins

            gp.memset(Qop[:].rearrange("p a h n -> p (a h n)").bitcast(F32), 0.0).then_inc(setup_pool, 1)
            gp.memset(MX[:], 0.0).then_inc(setup_pool, 1)
            gp.memset(Vp[:], 0.0).then_inc(setup_pool, 1)
            pool.wait_ge(setup_pool, 3)
            for v in range(2):
                gp.memset(Vp[:, :, :, v:H:2, 16 * v + HD:16 * v + HD + 1]
                          .rearrange("p a q h o -> p (a q) (h o)"), 1.0).then_inc(setup_pool, 1)
            pool.wait_ge(setup_dve, 2)
            pool.wait_ge(consts_in, CONSTS * 16)

            for sl in slots(pool):
                ch.enter(sl)
                A, B, C, V, Z = sl.A, sl.B, sl.C, sl.V, sl.Dn
                if C is not None:
                    split_max(C, 1)
                if Z is not None:
                    pool.wait_ge(wd_in, Z.l * 160 + 160)
                    if Z.full and Z.b > 0:
                        pool.wait_ge(y_used, Z.t)
                    elif sl.s >= 2 or sl.reg is not None:
                        pool.wait_ge(y2_used, Z.t)
                    if Z.full:
                        gp.tensor_copy(HB[:], rows(BO)).then_inc(hb_done, 1)
                    else:
                        gp.tensor_tensor(HB[:], Hh[:, Z.b], rows(BO), ALU.add).then_inc(hb_done, 1)
                    pool.wait_ge(rec_done, Z.t + 1)
                    if sl.s >= 2 or sl.reg is not None:
                        pool.wait_ge(y_filled, Z.t)
                    gp.tensor_tensor(ATT[:], NUM[:], DEN[:], ALU.mult).then_inc(att_done, 1)
                if A is not None:
                    for x in range(2):
                        pool.wait_ge(r1_done, A.t * 2 + 1 + x)
                        ch.link(gp.tensor_copy(XS[:, x, 1, :], R1[:, x, :]))
                        gp.tensor_tensor(XS[:, x, 2, :], R1[:, x, :], XS[:, x, 1, :], ALU.subtract) \
                            .then_inc(parts_done, 1)
                if C is not None and not C.full:
                    pool.wait_ge(em_in, C.t * 16 + 16)
                    if sl.s >= 1:
                        pool.wait_ge(den_done, C.t)
                    gp.tensor_tensor(DN[:], NMQ[:], EM[:], ALU.mult).then_inc(dn_done, 1)
                if Z is not None:
                    inverse_std(Z, 0)
                    if sl.s >= 2 or sl.reg is not None:
                        pool.wait_ge(h1t_filled, Z.t)
                    if Z.full:
                        if Z.b > 0:
                            pool.wait_ge(out_done, 16 * Z.b)
                        affine(Z, 0, G1, BE1, H1[:], Hh[:, Z.b]).then_inc(h1_done, 1)
                    else:
                        affine(Z, 0, G1, BE1, H1[:]).then_inc(h1_done, 1)
                        pool.wait_ge(h1_done, Z.t + 1)
                        gp.tensor_tensor(HB[:], H1[:], rows(B2), ALU.add).then_inc(h1b_done, 1)
                if V is not None:
                    pool.wait_ge(v_done, V.t + 1)
                    if sl.s >= 1:
                        pool.wait_ge(pv_done, Z.pbase() + (16 if Z.full else 4))
                    vc = VC[:].rearrange("p q (h v e) -> p (q h) v e", v=2, e=HD)
                    vp = Vp[:, V.par].rearrange("p q (h v) e -> p (q h) v e", v=2)
                    for v in range(2):
                        ins = gp.tensor_copy(vp[:, :, v, 16 * v:16 * v + HD], vc[:, :, v, :])
                    ins.then_inc(vp_done, 1)
                if B is not None:
                    split_max(B, 0)
                if Z is not None:
                    inverse_std(Z, 1)
                    if Z.full:
                        affine(Z, 1, G2, BE2, X[:], H1[:], Hh[:, Z.b]).then_inc(z_done, 1)
                        inverse_std(Z, 2)
                    elif Z.last:
                        affine(Z, 1, G2, BE2, X[:]).then_inc(x2_done, 1)
                        inverse_std(Z, 2)
                        pool.wait_ge(xr_in, Z.b * 16 + 16)
                        affine(Z, 2, GF, BF, X[:], XR[:]).then_inc(lnf_done, 1)
                        inverse_std(Z, 3)
                    else:
                        affine(Z, 1, G2, BE2, Hh[:, Z.b]).then_inc(h2_done, 1)
            ch.enter(Slot(NITEMS + 1))


def constants():
    def bf(a):
        return (np.ascontiguousarray(a, np.float32).view(np.uint32) >> 16).astype(np.uint16)

    pos = np.arange(S)
    level = np.frexp((pos + 1).astype(np.float64))[1] - 1
    coord = (pos >> level) / 2.0 ** level
    div = np.exp(np.arange(0, D, 2, dtype=np.float64) * -(np.log(10000.0) / D))
    ang = pos[:, None].astype(np.float64) * div[None, :]
    pe = np.zeros((S, D), np.float32)
    pe[:, 0::2] = (np.sin(ang) * coord[:, None]).astype(np.float32)
    pe[:, 1::2] = (np.cos(ang) * coord[:, None]).astype(np.float32)
    masked = (pos[:, None] & pos[None, :]) != 0
    count = masked.sum(0).astype(np.float32)
    floor = np.where(count > 0, 0.0, 3e38).astype(np.float32).reshape(QT, P).T
    bits = ((pos[None, :] >> np.arange(9)[:, None]) & 1).astype(np.float32)
    sel = np.zeros((4, P, P), np.float32)
    for h in range(H):
        u, c, v = h // HALF, h % HALF // 2, h % 2
        for e in range(HD):
            sel[u, 32 * c + 16 * v + e, HD * h + e] = 1
            sel[2 + u, 32 * c + 16 * v + HD, HD * h + e] = 1
    tri = (np.arange(NE)[None, :] < np.arange(NE)[:, None]).astype(np.float32)
    return {
        "c_pos": pe,
        "c_idf": np.eye(P, dtype=np.float32),
        "c_idb": bf(np.eye(P)),
        "c_nfloor": np.ascontiguousarray(np.repeat(floor[:, :, None], HALF, 2).reshape(P, QT * HALF)),
        "c_krows": bf(np.concatenate([bits, np.ones((3, S), np.float32)])),
        "c_qrows": bf(-BIG * bits),
        "c_zero": bf(np.zeros((12, HALF * S))),
        "c_notm": masked.astype(np.float32),
        "c_nmq": count,
        "c_sel": sel.reshape(4 * P, P),
        "c_tri": np.ascontiguousarray(np.broadcast_to(tri.reshape(1, NE * NE), (P, NE * NE))),
    }


_INS = ["L0_attn_" + n for n in ("x", "Wq", "bq", "Wk", "bk", "Wv", "bv", "Wo", "bo", "W1", "b1", "W2", "b2",
                                 "ln1_g", "ln1_b", "ln2_g", "ln2_b", "lnf_g", "lnf_b")] + \
       ["L0_ffn_" + n for n in ("Wq", "bq", "Wk", "bk", "Wv", "bv", "Wo", "bo", "g1", "be1", "g2", "be2",
                                "Wg", "bg", "We", "bexp")]


def kernel(**inputs):
    import concourse.bacc as _bacc
    from concourse import mybir as _mybir
    from concourse.bass_utils import run_bass_kernel_spmd as _run

    nc = _bacc.Bacc("TRN2", target_bir_lowering=False, num_devices=1)
    arrays = {n: np.ascontiguousarray(inputs[n]) for n in _INS}
    arrays.update(constants())
    d = {n: nc.dram_tensor(n, a.shape, _mybir.dt.from_np(a.dtype), kind="ExternalInput").ap()
         for n, a in arrays.items()}
    for n in ("c_idb", "c_krows", "c_qrows", "c_zero"):
        d[n] = d[n].bitcast(BF16)
    out = nc.dram_tensor("out", (NB, S, D), F32, kind="ExternalOutput").ap()
    build(nc, d, out)
    r = _run(nc, [arrays], core_ids=[0])
    return r.results[0]["out"]
```

```python
import numpy as np
from contextlib import ExitStack

import concourse.bass as bass
from concourse import mybir

F32 = mybir.dt.float32
BF16 = mybir.dt.bfloat16
I32 = mybir.dt.int32
ALU = mybir.AluOpType
ACT = mybir.ActivationFunctionType
AX = mybir.AxisListType

P = 128
NB, S, D = 4, 512, 128
H, HD = 16, 8
L, HID = 6, 512
NE = 8
QT = S // P
HALF = H // 2
SCALE = float(np.float32(1.0) / np.sqrt(np.float32(HD)))
EPS = 1e-5
BIG = float(2.0 ** 100)
NMASKED = NB * L
NITEMS = NMASKED + NB
STEPS = 36
PIECES = {1: [0], 2: [1, 2], 3: [3]}
WP_STEPS = (15, 17)
WP_TILES = ((0, 1), (2, 3))
WP_SUMS = ((9, None), (7, 4), (6, 5), (0, 8))
W1_STEPS = (22, 23, 24, 24)
GELUS = ({23: (0, 1, 2, 3)}, {23: (0, 1), 25: (2, 3)})
W2_STEPS = (25, 26, 27, 28)
EX_STEPS = (24, 25, 30, 31, 32, 33, 34, 35)
DVE_STEPS, POOL_STEPS = 4 * 6, 4 * 9
CONSTS = 8
RATES_SP = (4, 8, 64, 128, 144, 192, 384)
RATES_PE = (4, 8, 16, 32, 64, 144, 160, 192)
RATES_ACT = (4, 8, 16, 64, 144, 384)
RATES_DVE = (4, 8, 24, 64, 128, 144)
RATES_POOL = (4, 8, 16, 36, 64, 160)
UM, UF = 36, 64
PARTS_Q = ((0, 3), (1, 2), (2, 1))
PARTS_K = ((0, 3), (0, 2), (0, 1))
ALLOWED = [[0, 1, 2, 3], [0, 2], [0, 1], [0]]


class Lin:

    def __init__(self, c, k):
        self.c, self.k = c, k

    def __add__(self, n):
        return Lin(self.c, self.k + n)

    __radd__ = __add__

    def __sub__(self, n):
        return Lin(self.c, self.k - n)

    def __mul__(self, n):
        return Lin(self.c * n, self.k * n)

    __rmul__ = __mul__


class Queue:

    def __init__(self, eng, rates, passed=None):
        self.eng, self.rates, self.passed = eng, rates, passed
        self.value = eng.alloc_register("wait_value")
        self.multiple = {c: eng.alloc_register(f"times_{c}") for c in rates}
        self.i = None

    def layers(self, n):
        with self.eng.Fori(0, n) as i:
            self.i = i
            for c in self.rates:
                self.eng.reg_mul(self.multiple[c], self.eng.to_reg(i), c)
            yield
        self.i = None

    def wait_ge(self, sem, value):
        if isinstance(value, Lin):
            if value.k == 0:
                value = self.multiple[value.c]
            else:
                self.eng.reg_add(self.value, self.multiple[value.c], value.k)
                value = self.value
            self.eng.wait_ge(sem, value)
            if self.passed is not None:
                self.eng.sem_inc(self.passed, 1)
            return
        self.eng.wait_ge(sem, value)

    def dma_start(self, out, in_):
        return self.eng.dma_start(out, in_)


class Item:

    def __init__(self, t, b, l, full):
        self.t, self.b, self.l, self.full = t, b, l, full
        self.par = b % 2
        self.last = False

    def units(self):
        return UF if self.full else UM

    def ubase(self):
        return NMASKED * UM + (self.t - NMASKED) * UF if self.full else self.t * UM

    def pbase(self):
        return NMASKED * 4 + (self.t - NMASKED) * 16 if self.full else self.t * 4


def item_at(s, k, reg=None):
    j = s + k
    if reg is None:
        if not 0 <= j < NITEMS:
            return None
        it = Item(j, j % NB, j // NB, j >= NMASKED)
        it.last = NMASKED - NB <= j < NMASKED
        return it
    return Item(Lin(NB, j), j % NB, Lin(1, j // NB), False)


class Slot:
    def __init__(self, s, reg=None):
        self.s, self.reg = s, reg
        self.A, self.B, self.C, self.Dn = (item_at(s, k, reg) for k in (2, 1, 0, -1))
        self.V = self.B

    def before(self):
        return Slot(self.s - 1, self.reg)


def slots(eng):
    for s in (-2, -1, 0):
        yield Slot(s)
    for _ in eng.layers(L - 1):
        for s in range(1, 1 + NB):
            yield Slot(s, True)
    for s in range(1 + NB * (L - 1), NITEMS + 1):
        yield Slot(s)


class Chain:

    def __init__(self, eng, sem, per_loop):
        self.eng, self.sem, self.per = eng, sem, per_loop
        self.n, self.start, self.reg = 0, None, None

    def enter(self, slot):
        if slot.reg is not None and self.reg is None:
            self.start, self.reg = self.n, slot.reg
        if slot.reg is None and self.reg is not None:
            assert self.n - self.start == self.per, (self.n - self.start, self.per)
            self.n += self.per * (L - 2)
            self.reg = None

    def inc(self, ins):
        ins.then_inc(self.sem, 1)
        self.n += 1

    def wait(self):
        self.eng.wait_ge(self.sem, self.n if self.reg is None else Lin(self.per, self.n))

    def link(self, ins):
        self.inc(ins)
        self.wait()


def unit_blocks(full, i):
    if full:
        return i // 4, [i % 4], ALLOWED[0]
    if i < 4:
        return 0, [i], ALLOWED[0]
    if i < 8:
        return (i - 2) // 2, [2 * (i % 2), 2 * (i % 2) + 1], ALLOWED[(i - 2) // 2]
    return 3, [0, 1, 2, 3], ALLOWED[3]


def layer(q, l):
    return q.i + l.k if isinstance(l, Lin) else l


def head_of(g, c):
    return HALF * (g // 2) + 2 * c + g % 2


def pick(ap, blocks):
    v = ap.rearrange("p (a n) -> p a n", n=P)
    if blocks == [0, 2]:
        return v[:, 0:3:2, :]
    return v[:, 0:len(blocks), :]


def build(nc, d, out):
    with ExitStack() as ctx:
        def sb(name, shape, dt=F32):
            return ctx.enter_context(nc.sbuf_tensor(name, shape, dt))

        def pb(name, shape, dt=F32):
            return ctx.enter_context(nc.psum_tensor(name, shape, dt))

        sems = {}

        def sem(name):
            sems[name] = ctx.enter_context(nc.semaphore(name))
            return sems[name]

        Qop = sb("Qop", [P, 2, H, S], BF16)
        Kop = sb("Kop", [P, 2, H, S], BF16)
        XS = sb("XS", [P, 2, 3, S], BF16)
        R1 = sb("R1", [P, 2, S])
        Vp = sb("Vp", [P, 2, QT, H, 32])
        PT = sb("PT", [P, 18, S])
        AU = sb("AU", [P, 2, S])
        LOWM = sb("LOWM", [P, P])
        ONES = sb("ONES", [P, P])
        NMQ = sb("NMQ", [P, S])
        NFLOOR = sb("NFLOOR", [P, QT, HALF])
        IDF = sb("IDF", [P, P])
        IDB = sb("IDB", [P, P], BF16)
        SEL = sb("SEL", [P, 4, P])
        MX = sb("MX", [P, 2, QT, HALF])
        NM = sb("NM", [P, 2, QT, HALF])
        MR = sb("MR", [P, 2, QT, HALF])
        SPL = sb("SPL", [P, 2, QT, 3, HALF], BF16)
        MROW = sb("MROW", [3 * HALF, 2, S], BF16)
        EXM = sb("EXM", [P, QT, H])
        ER = sb("ER", [H, S])
        EM = sb("EM", [P, S])
        NUM = sb("NUM", [P, S])
        DN = sb("DN", [P, S])
        DEN = sb("DEN", [P, S])
        ATT = sb("ATT", [P, S])
        Hh = sb("Hh", [P, NB, QT, D])
        HT = sb("HT", [P, NB, S])
        HB = sb("HB", [P, QT, D])
        VS = sb("VS", [P, 10, D])
        VC = VS[:, 0:QT]
        X = sb("X", [P, QT, D])
        XN = sb("XN", [P, QT, D])
        H1 = sb("H1", [P, QT, D])
        H1T = sb("H1T", [P, S])
        HIDT = sb("HIDT", [P, QT, S])
        XR = sb("XR", [P, QT, D])
        BS = sb("BS", [P, QT, 6])
        MV = sb("MV", [P, QT, 2])
        VE = sb("VE", [P, QT])
        RS = sb("RS", [P, QT])
        NMEAN = sb("NMEAN", [P, QT])
        MHALF = sb("MHALF", [P, QT])
        Wq, Wk, Wv, Wo = (sb(n, [P, D]) for n in ("Wq", "Wk", "Wv", "Wo"))
        bqk = sb("bqk", [P, 2])
        BV = sb("BV", [P, D])
        W1 = sb("W1", [P, HID])
        W2 = sb("W2", [P, HID // P, D])
        b1 = sb("b1", [P, HID // P])
        BO, G1, BE1, B2, G2, BE2, GF, BF = (sb(n, [P, D]) for n in
                                            ("BO", "G1", "BE1", "B2", "G2", "BE2", "GF", "BF"))
        WG = sb("WG", [P, NE])
        BG = sb("BG", [P, NE])
        TRI = sb("TRI", [P, NE, NE])
        LG = sb("LG", [P, QT, NE])
        LM = sb("LM", [P, QT])
        PR = sb("PR", [P, QT, NE])
        WT = sb("WT", [P, QT, NE])
        WE = HIDT[:, 0:2, :].rearrange("p a n -> p (a n)")
        BEXP = HIDT[:, 2:4, :].rearrange("p a n -> p (a n)")
        YE = sb("YE", [P, S])[:]
        GT, EQ = (sb(n, [P, QT, NE, NE])[:] for n in ("GT", "EQ"))

        pS = pb("pS", [P, 2, S])
        pT = pb("pT", [P, 2, S])
        pV = pb("pV", [P, 2, S])
        pD = pb("pD", [P, 2, S])

        Qs = nc.dram_tensor("Qs", (H, HD, 6, S), BF16)[:]
        Ks = nc.dram_tensor("Ks", (H, HD, 6, S), BF16)[:]
        Ms = nc.dram_tensor("Ms", (2, 3, HALF, S), BF16)[:]
        Es = nc.dram_tensor("Es", (H, HD, S), F32)[:]

        consts_in = sem("consts_in")
        pos_in = sem("pos_in")
        x_in = sem("x_in")
        posin = sem("posin")
        ht0_filled = sem("ht0_filled")
        ht0_copied = sem("ht0_copied")
        setup_pool = sem("setup_pool")
        setup_dve = sem("setup_dve")
        opconst = sem("opconst")
        wa_in = sem("wa_in")
        wv_in = sem("wv_in")
        wd_in = sem("wd_in")
        we_in = sem("we_in")
        qk_filled = sem("qk_filled")
        hi_done = sem("hi_done")
        r1_done = sem("r1_done")
        mid_done = sem("mid_done")
        parts_done = sem("parts_done")
        parts_out = sem("parts_out")
        placed = [sem("placed0"), sem("placed1")]
        s_filled = sem("s_filled")
        s_used = sem("s_used")
        nm_done = sem("nm_done")
        mparts_done = sem("mparts_done")
        m_filled = sem("m_filled")
        m_copied = sem("m_copied")
        m_out = sem("m_out")
        m_placed = [sem("m_placed0"), sem("m_placed1")]
        exm_done = sem("exm_done")
        e_filled = sem("e_filled")
        e_copied = sem("e_copied")
        e_out = sem("e_out")
        em_in = sem("em_in")
        tw_done = sem("tw_done")
        v_filled = sem("v_filled")
        v_done = sem("v_done")
        vs_done = sem("vs_done")
        vp_done = sem("vp_done")
        t_filled = sem("t_filled")
        t_used = sem("t_used")
        pv_done = sem("pv_done")
        au_copied = sem("au_copied")
        wp_filled = sem("wp_filled")
        num_filled = sem("num_filled")
        den_filled = sem("den_filled")
        dn_done = sem("dn_done")
        num_done = sem("num_done")
        den_done = sem("den_done")
        rec_done = sem("rec_done")
        att_done = sem("att_done")
        hb_done = sem("hb_done")
        y_filled = sem("y_filled")
        y_used = sem("y_used")
        ln_st = sem("ln_st")
        ln_rs = sem("ln_rs")
        ln_xn = sem("ln_xn")
        h1_done = sem("h1_done")
        h1b_done = sem("h1b_done")
        h1t_filled = sem("h1t_filled")
        h1t_copied = sem("h1t_copied")
        hid_filled = sem("hid_filled")
        gelu_done = sem("gelu_done")
        y2_filled = sem("y2_filled")
        y2_used = sem("y2_used")
        h2_done = sem("h2_done")
        x2_done = sem("x2_done")
        lnf_done = sem("lnf_done")
        xr_in = sem("xr_in")
        ht_filled = sem("ht_filled")
        ht_copied = sem("ht_copied")
        gate_filled = sem("gate_filled")
        lg_done = sem("lg_done")
        pe_done = sem("pe_done")
        ex_filled = sem("ex_filled")
        ex_used = sem("ex_used")
        moe_done = sem("moe_done")
        z_done = sem("z_done")
        out_ready = sem("out_ready")
        out_done = sem("out_done")
        sp_passed, pool_passed, dve_passed = sem("sp_passed"), sem("pool_passed"), sem("dve_passed")
        dve_step = sem("dve_step")
        pool_step = sem("pool_step")

        def ln_no(it, k):
            if it.full:
                return 2 * (NMASKED - NB) + 4 * NB + 3 * (it.t - NMASKED) + k
            if it.last:
                return 2 * (NMASKED - NB) + 4 * (it.t - (NMASKED - NB)) + k
            return it.t * 2 + k

        def xn_no(it, k):
            return 2 * NB + it.t - NMASKED if it.full else 2 * (it.t - (NMASKED - NB)) + k - 1

        def bank_order(sl):
            A, B, C, V, Z = sl.A, sl.B, sl.C, sl.V, sl.Dn
            masked = Z is not None and not Z.full
            full = Z is not None and Z.full
            b0 = [
                ("M1", C is not None, m_copied, C and C.t * 2 + 2),
                ("DEN", Z is not None, den_done, Z and Z.t + 1),
                ("K", A is not None, r1_done, A and A.t * 2 + 2),
                ("WP", C is not None and not C.full, tw_done, C and C.t + 1),
                ("V", V is not None, v_done, V and V.t + 1),
                ("W1_1", masked, gelu_done, Z and Z.t * 4 + 2),
                ("W1_3", masked, gelu_done, Z and Z.t * 4 + 4),
                ("GATE", full, lg_done, Z and full and Z.t - NMASKED + 1),
                ("X0", full, ex_used, full and (Z.t - NMASKED) * 8 + 1),
                ("M0", B is not None, m_copied, B and B.t * 2 + 1),
            ] + [(f"X{i}", full, ex_used, full and (Z.t - NMASKED) * 8 + i + 1) for i in (2, 4, 6)] + [
                ("T2", masked, ht_copied, Z and Z.t + 1),
            ]
            b1_ = [
                ("E", C is not None and not C.full, e_copied, C and C.t + 1),
                ("NUM", Z is not None, num_done, Z and Z.t + 1),
                ("Q", A is not None, r1_done, A and A.t * 2 + 1),
                ("WO", Z is not None, y_used, Z and Z.t + 1),
                ("T1", Z is not None, h1t_copied, Z and Z.t + 1),
                ("W1_0", masked, gelu_done, Z and Z.t * 4 + 1),
                ("W1_2", masked, gelu_done, Z and Z.t * 4 + 3),
            ] + [(f"X{i}", full, ex_used, full and (Z.t - NMASKED) * 8 + i + 1) for i in (1, 3, 5, 7)] + [
                ("W2", masked, y2_used, Z and Z.t + 1),
            ]
            return b0, b1_

        def bank_for(pe, sl, name):
            for bank in (0, 1):
                order = bank_order(sl)[bank]
                names = [o[0] for o in order]
                if name not in names:
                    continue
                k = names.index(name)
                look = sl
                for _ in range(4):
                    for o in reversed(order[:k]):
                        if o[1]:
                            pe.wait_ge(o[2], o[3])
                            return pD[:, bank, :]
                    if look.s <= -2:
                        return pD[:, bank, :]
                    look = look.before()
                    order = bank_order(look)[bank]
                    k = len(order)
                return pD[:, bank, :]

        def step_units(it, step):
            n = it.units()
            return range((step * n + STEPS - 1) // STEPS, ((step + 1) * n + STEPS - 1) // STEPS)

        block = ctx.enter_context(nc.Block())

        @block.sync
        def _(sp_engine):
            sp = Queue(sp_engine, RATES_SP, sp_passed)
            def load_a(l, names=("L0_attn_Wq", "L0_attn_Wk", "L0_attn_bq", "L0_attn_bk")):
                wq, wk, bq, bk = ((d[n][l] if l is not None else d[n]) for n in names)
                sp.dma_start(Wq[:], wq).then_inc(wa_in, 16)
                sp.dma_start(Wk[:], wk).then_inc(wa_in, 16)
                sp.dma_start(bqk[:, 0:1], bq.rearrange("(p o) -> p o", o=1)).then_inc(wa_in, 16)
                sp.dma_start(bqk[:, 1:2], bk.rearrange("(p o) -> p o", o=1)).then_inc(wa_in, 16)

            def bcast(dst, row, s):
                sp.dma_start(dst, row.rearrange("(o n) -> o n", o=1).to_broadcast([P, D])).then_inc(s, 16)

            def load_v(l, pre="L0_attn_"):
                w, b = ((d[pre + n][l] if l is not None else d[pre + n]) for n in ("Wv", "bv"))
                sp.dma_start(Wv[:], w).then_inc(wv_in, 16)
                bcast(BV[:], b, wv_in)

            def load_d(l):
                sp.dma_start(Wo[:], d["L0_attn_Wo"][l]).then_inc(wd_in, 16)
                sp.dma_start(W1[:], d["L0_attn_W1"][l]).then_inc(wd_in, 16)
                sp.dma_start(W2[:], d["L0_attn_W2"][l].rearrange("(p j) n -> p j n", p=P)).then_inc(wd_in, 16)
                sp.dma_start(b1[:], d["L0_attn_b1"][l].rearrange("(p j) -> p j", p=P)).then_inc(wd_in, 16)
                for t, n in ((BO, "bo"), (G1, "ln1_g"), (BE1, "ln1_b"), (B2, "b2"), (G2, "ln2_g"), (BE2, "ln2_b")):
                    bcast(t[:], d["L0_attn_" + n][l], wd_in)

            def load_experts():
                sp.dma_start(Wo[:], d["L0_ffn_Wo"]).then_inc(wd_in, 16)
                for t, n in ((BO, "bo"), (G1, "g1"), (BE1, "be1"), (G2, "g2"), (BE2, "be2")):
                    bcast(t[:], d["L0_ffn_" + n], wd_in)
                sp.dma_start(WG[:], d["L0_ffn_Wg"]).then_inc(wd_in, 16)
                sp.dma_start(BG[:], d["L0_ffn_bg"].rearrange("(o n) -> o n", o=1).to_broadcast([P, NE])).then_inc(wd_in, 16)
                sp.dma_start(WE.rearrange("p (e n) -> p e n", e=NE),
                             d["L0_ffn_We"].rearrange("e p n -> p e n")).then_inc(wd_in, 16)
                sp.dma_start(BEXP, d["L0_ffn_bexp"].rearrange("e n -> (e n)").rearrange("(o n) -> o n", o=1)
                             .to_broadcast([P, NE * D])).then_inc(wd_in, 16)

            def store_parts(it):
                for x, dst, parts in ((0, Qs, PARTS_Q), (1, Ks, PARTS_K)):
                    sp.wait_ge(parts_done, it.t * 2 + 1 + x)
                    r = 0
                    for p0, n in parts:
                        src = (XS[:, x, p0:p0 + 1, :].to_broadcast([P, n, S]) if x == 0
                               else XS[:, x, p0:p0 + n, :])
                        sp.dma_start(dst.rearrange("h e r n -> (h e) r n")[:, r:r + n, :], src).then_inc(parts_out, 16)
                        r += n

            def place(it, u):
                hs = slice(HALF * u, HALF * (u + 1))
                for op, src in ((Qop, Qs), (Kop, Ks)):
                    sp.dma_start(op[0:48, it.par, hs, :],
                                 src[hs].rearrange("h e r n -> (e r) h n")).then_inc(placed[u], 16)
                z0 = 48 if it.full else 57
                sp.dma_start(Qop[z0:60, it.par, hs, :],
                             d["c_zero"][0:60 - z0].rearrange("p (h n) -> p h n", h=HALF)).then_inc(placed[u], 16)

            def shift_rows(it, u):
                sp.wait_ge(m_copied, it.t * 2 + 1 + u)
                sp.dma_start(Ms[u].rearrange("p h n -> (p h) n"), MROW[:, u, :]).then_inc(m_out, 16)
                sp.wait_ge(m_out, it.t * 32 + 16 * (u + 1))
                sp.dma_start(Qop[57:60, it.par, HALF * u:HALF * (u + 1), :], Ms[u]).then_inc(m_placed[u], 16)

            for b in range(NB):
                sp.dma_start(Hh[:, b], d["L0_attn_x"][b].rearrange("(q p) n -> p q n", p=P)).then_inc(x_in, 16)
                if b == 0:
                    sp.dma_start(XR[:], d["c_pos"].rearrange("(q p) n -> p q n", p=P)).then_inc(pos_in, 16)
                    sp.dma_start(IDF[:], d["c_idf"]).then_inc(pos_in, 16)
                    load_a(0)
            sp.dma_start(IDB[:], d["c_idb"]).then_inc(consts_in, 16)
            sp.dma_start(NFLOOR[:], d["c_nfloor"].rearrange("p (q h) -> p q h", q=QT)).then_inc(consts_in, 16)
            sp.wait_ge(setup_pool, 2)
            sp.wait_ge(setup_dve, 2)
            for par in range(2):
                sp.dma_start(Kop[48:60, par], d["c_krows"].rearrange("p (o n) -> p o n", o=1)
                             .to_broadcast([12, H, S])).then_inc(opconst, 16)
                sp.dma_start(Qop[48:57, par], d["c_qrows"].rearrange("p (o n) -> p o n", o=1)
                             .to_broadcast([9, H, S])).then_inc(opconst, 16)
            load_v(0)
            sp.dma_start(LOWM[:], d["c_lowm"]).then_inc(consts_in, 16)
            sp.dma_start(NMQ[:], d["c_nmq"].rearrange("(o n) -> o n", o=1).to_broadcast([P, S])).then_inc(consts_in, 16)
            sp.dma_start(SEL[:], d["c_sel"].rearrange("(k p) n -> p k n", p=P)).then_inc(consts_in, 16)
            sp.dma_start(TRI[:], d["c_tri"].rearrange("p (a b) -> p a b", a=NE)).then_inc(consts_in, 16)
            load_d(0)
            bcast(GF[:], d["L0_attn_lnf_g"], consts_in)
            bcast(BF[:], d["L0_attn_lnf_b"], consts_in)

            for sl in slots(sp):
                A, B, C, Z = sl.A, sl.B, sl.C, sl.Dn
                if B is not None:
                    if sl.s >= 1:
                        sp.wait_ge(t_filled, C.ubase())
                    sp.wait_ge(parts_out, B.t * 96 + 96)
                    place(B, 1)
                if C is not None:
                    shift_rows(C, 1)
                    if not C.full:
                        sp.wait_ge(e_copied, C.t + 1)
                        if sl.s >= 1:
                            sp.wait_ge(em_in, C.t * 16)
                        sp.dma_start(Es, ER[:, :].rearrange("h (o n) -> h o n", o=1)
                                     .to_broadcast([H, HD, S])).then_inc(e_out, 16)
                        sp.wait_ge(e_out, C.t * 16 + 16)
                        if sl.s >= 1:
                            sp.wait_ge(dn_done, C.t)
                            sp.wait_ge(tw_done, C.t)
                        sp.dma_start(EM[:], Es.rearrange("h e n -> (h e) n")).then_inc(em_in, 16)
                if A is not None:
                    if B is not None:
                        sp.wait_ge(placed[0], B.t * 48 + 48)
                        sp.wait_ge(placed[1], B.t * 48 + 48)
                    store_parts(A)
                    sp.wait_ge(parts_out, A.t * 96 + 96)
                    if C is not None:
                        sp.wait_ge(t_filled, C.ubase() + C.units() // 2)
                    else:
                        sp.wait_ge(opconst, 64)
                    place(A, 0)
                if Z is not None and Z.last:
                    if Z.b > 0:
                        sp.wait_ge(lnf_done, Z.b)
                    else:
                        sp.wait_ge(posin, NB)
                    sp.dma_start(XR[:], d["L0_attn_x"][Z.b].rearrange("(q p) n -> p q n", p=P)).then_inc(xr_in, 16)
                if B is not None:
                    shift_rows(B, 0)
                if A is not None and A.b == NB - 1 and (sl.reg is not None or A.l < L):
                    sp.wait_ge(r1_done, A.t * 2 + 2)
                    if sl.reg is None and A.l == L - 1:
                        load_a(None, ("L0_ffn_Wq", "L0_ffn_Wk", "L0_ffn_bq", "L0_ffn_bk"))
                    else:
                        load_a(layer(sp, A.l + 1))
                if B is not None and B.b == NB - 1 and (sl.reg is not None or B.l < L):
                    sp.wait_ge(v_done, B.t + 1)
                    if sl.reg is None and B.l == L - 1:
                        load_v(None, "L0_ffn_")
                    else:
                        load_v(layer(sp, B.l + 1))
                if Z is not None and Z.b == NB - 1 and not Z.full:
                    sp.wait_ge(ht_copied, Z.t + 1)
                    if Z.last:
                        load_experts()
                    else:
                        load_d(layer(sp, Z.l + 1))
                if Z is not None and Z.full:
                    sp.wait_ge(out_ready, Z.t - NMASKED + 1)
                    sp.dma_start(out[Z.b].rearrange("(q p) n -> p q n", p=P), H1[:]).then_inc(out_done, 16)
            sp.wait_ge(out_done, 16 * NB)

        @block.tensor
        def _(pe_engine):
            pe = Queue(pe_engine, RATES_PE)
            mm = nc.tensor.matmul

            def score_unit(it, k, maxima):
                n = it.ubase() + k
                g, i = divmod(k, 16 if it.full else 9)
                tile, heads, blocks = unit_blocks(it.full, i)
                u = g // 2
                if maxima:
                    if i == 0 and g % 2 == 0:
                        pe.wait_ge(placed[u], it.t * 48 + 48)
                    filled, used, bank = s_filled, s_used, pS[:, k % 2, :]
                    st, mv = Qop, Kop
                else:
                    if i == 0 and g % 2 == 0:
                        pe.wait_ge(m_placed[u], it.t * 16 + 16)
                    filled, used, bank = t_filled, t_used, pT[:, k % 2, :]
                    st, mv = Kop, Qop
                if not (isinstance(n, int) and n < 2):
                    pe.wait_ge(used, n - 1)
                w = P * len(blocks)
                for x, c in enumerate(heads):
                    h = head_of(g, c)
                    ins = mm(bank[:, x * w:(x + 1) * w], st[:, it.par, h, tile * P:(tile + 1) * P],
                             pick(mv[:, it.par, h, :], blocks), start=True, stop=True)
                ins.then_inc(filled, 1)

            def value_product(it, g, tiles):
                u, v = divmod(g, 2)
                if v == 0 and tiles[0] == 0 and not (isinstance(it.t, int) and it.t == 0):
                    pe.wait_ge(au_copied, it.t * 2 - 1 + u)
                if g == 0 and tiles[0] == 0:
                    pe.wait_ge(vp_done, it.t + 1)
                if it.full:
                    pe.wait_ge(t_used, it.ubase() + 16 * g + 4 * tiles[0] + 4)
                elif tiles[0] == 0:
                    pe.wait_ge(t_used, it.ubase() + 9 * g + 9)
                for kt in tiles:
                    for c in range(4):
                        h = head_of(g, c)
                        if it.full:
                            src = PT[:, 4 * kt + c, :]
                            blocks = ALLOWED[0]
                        else:
                            blocks = ALLOWED[kt]
                            w = P * len(blocks)
                            for i in range(9):
                                tile, heads, _ = unit_blocks(False, i)
                                if tile == kt and c in heads:
                                    x = heads.index(c)
                                    src = PT[:, 9 * (g % 2) + i, x * w:(x + 1) * w]
                        first = v == 0 and kt == 0
                        last = v == 1 and kt == 3
                        ins = mm(pick(pV[32 * c:32 * c + 32, u, :], blocks),
                                 Vp[:, it.par, kt, h, :], src, start=first, stop=last, skip_group_check=True,
                                 tile_position=(0, 32 * c))
                if it.full or tiles[-1] == QT - 1:
                    ins.then_inc(pv_done, 1)

            def transposes(bank, src, ident, rows):
                for q in range(QT):
                    ins = nc.tensor.transpose(bank[0:rows, q * P:(q + 1) * P], src(q), ident)
                return ins

            def shift_transpose(sl, it, u):
                pe.wait_ge(mparts_done, it.t * 2 + 1 + u)
                bank = bank_for(pe, sl, "M1" if u else "M0").bitcast(BF16)
                transposes(bank, lambda q: SPL[:, u, q].rearrange("p a h -> p (a h)"), IDB[:], 3 * HALF) \
                    .then_inc(m_filled, 1)

            pe.wait_ge(pos_in, 32)
            for b in range(NB):
                pe.wait_ge(posin, b + 1)
                if b >= 2:
                    pe.wait_ge(ht0_copied, b - 1)
                transposes(pD[:, b % 2, :], lambda q: Hh[:, b, q, :], IDF[:], P).then_inc(ht0_filled, 1)
            pe.wait_ge(ht0_copied, NB)

            for sl in slots(pe):
                A, B, C, V, Z = sl.A, sl.B, sl.C, sl.V, sl.Dn
                prev_last = Z is not None
                if sl.s == -1 and sl.reg is None:
                    pe.wait_ge(consts_in, CONSTS * 16)
                if C is not None and C.full and C.b == 0:
                    value_product(Z, 3, range(QT))
                    prev_last = False
                for step in range(STEPS):
                    if B is not None:
                        for k in step_units(B, step):
                            score_unit(B, k, True)
                    if C is not None:
                        for k in step_units(C, step):
                            score_unit(C, k, False)
                            if C.full and k % 4 == 1 and k >= 5:
                                qd = k // 4 - 1
                                value_product(C, qd // 4, [qd % 4])
                    if prev_last and step in ((1,) if Z.full else (0, 1, 2)):
                        value_product(Z, 3, [3] if Z.full else PIECES[step + 1])
                    for g, first_step in ((0, 10), (1, 25), (2, 29)):
                        if C is not None and not C.full and step - first_step + 1 in PIECES:
                            value_product(C, g, PIECES[step - first_step + 1])
                    if step == 3 and C is not None:
                        shift_transpose(sl, C, 1)
                    if step == 5 and C is not None and not C.full:
                        pe.wait_ge(exm_done, C.t + 1)
                        bank = bank_for(pe, sl, "E")
                        transposes(bank, lambda q: EXM[:, q, :], IDF[:], H).then_inc(e_filled, 1)
                    if step in (6, 7) and Z is not None:
                        if step == 6:
                            pe.wait_ge(au_copied, Z.t * 2 + 2)
                        bank = bank_for(pe, sl, "NUM" if step == 6 else "DEN")
                        for c in range(4):
                            u, cols = c // 2, slice(32 * c, 32 * c + 32)
                            ins = mm(bank[cols, :], SEL[:, (0 if step == 6 else 2) + u, cols], AU[:, u, :],
                                     start=True, stop=True, tile_position=(0, 32 * c))
                        ins.then_inc(num_filled if step == 6 else den_filled, 1)
                    if step in (9, 11) and A is not None:
                        if step == 9:
                            pe.wait_ge(wa_in, A.l * 64 + 64)
                            if sl.s >= 2 or sl.reg is not None:
                                pe.wait_ge(ht_copied, A.t - NB + 1)
                        bank = bank_for(pe, sl, "Q" if step == 9 else "K")
                        mm(bank, (Wq if step == 9 else Wk)[:], HT[:, A.b, :], start=True, stop=True) \
                            .then_inc(qk_filled, 1)
                    if step == 14 and Z is not None:
                        pe.wait_ge(att_done, Z.t + 1)
                        pe.wait_ge(wd_in, Z.l * 160 + 160)
                        bank = bank_for(pe, sl, "WO")
                        for q in range(QT):
                            ins = mm(bank[:, q * P:(q + 1) * P], ATT[:, q * P:(q + 1) * P], Wo[:],
                                     start=True, stop=True)
                        ins.then_inc(y_filled, 1)
                    if step in WP_STEPS and C is not None and not C.full:
                        n = WP_STEPS.index(step)
                        if n == 0:
                            pe.wait_ge(vs_done, C.t + 1)
                            wp_bank = bank_for(pe, sl, "WP")
                        for q in WP_TILES[n]:
                            part, whole = WP_SUMS[q]
                            ins = mm(wp_bank[:, q * P:(q + 1) * P], VS[:, part, :], LOWM[:], start=True,
                                     stop=whole is None)
                            if whole is not None:
                                ins = mm(wp_bank[:, q * P:(q + 1) * P], VS[:, whole, :], ONES[:], start=False,
                                         stop=True)
                        if n == len(WP_STEPS) - 1:
                            ins.then_inc(wp_filled, 1)
                    if step == 20 and Z is not None:
                        pe.wait_ge(h1_done, Z.t + 1)
                        bank = bank_for(pe, sl, "T1")
                        transposes(bank, lambda q: H1[:, q, :], IDF[:], P).then_inc(h1t_filled, 1)
                    if step == 21 and V is not None:
                        pe.wait_ge(wv_in, V.l * 32 + 32)
                        bank = bank_for(pe, sl, "V")
                        for q in range(QT):
                            ins = mm(bank[:, q * P:(q + 1) * P], HT[:, V.b, q * P:(q + 1) * P], Wv[:],
                                     start=True, stop=True)
                        ins.then_inc(v_filled, 1)
                    for j in range(HID // P):
                        if step == W1_STEPS[j] and Z is not None and not Z.full:
                            if j == 0:
                                pe.wait_ge(h1t_copied, Z.t + 1)
                            bank = bank_for(pe, sl, f"W1_{j}")
                            mm(bank, W1[:, j:HID:HID // P], H1T[:], start=True, stop=True).then_inc(hid_filled, 1)
                    if step == 23 and Z is not None and Z.full:
                        pe.wait_ge(h1t_copied, Z.t + 1)
                        bank = bank_for(pe, sl, "GATE")
                        for q in range(QT):
                            ins = mm(bank[:, q * NE:(q + 1) * NE], H1T[:, q * P:(q + 1) * P], WG[:],
                                     start=True, stop=True)
                        ins.then_inc(gate_filled, 1)
                    if step == 28 and B is not None:
                        shift_transpose(sl, B, 0)
                    if step in EX_STEPS and Z is not None and Z.full:
                        i = EX_STEPS.index(step)
                        q, e0 = divmod(i, 2)
                        bank = bank_for(pe, sl, f"X{i}")
                        mm(bank, H1T[:, q * P:(q + 1) * P], WE[:, e0 * S:(e0 + 1) * S],
                           start=True, stop=True).then_inc(ex_filled, 1)
                    if step in W2_STEPS and Z is not None and not Z.full:
                        q = W2_STEPS.index(step)
                        if q == 0:
                            pe.wait_ge(gelu_done, Z.t * 4 + 4)
                            w2_bank = bank_for(pe, sl, "W2")
                        for j in range(HID // P):
                            ins = mm(w2_bank[:, q * P:(q + 1) * P], HIDT[:, j, q * P:(q + 1) * P], W2[:, j, :],
                                     start=j == 0, stop=j == HID // P - 1)
                        if q == QT - 1:
                            ins.then_inc(y2_filled, 1)
                    if step == STEPS - 1 and Z is not None and not Z.full:
                        pe.wait_ge(h2_done, Z.t + 1)
                        bank = bank_for(pe, sl, "T2")
                        transposes(bank, lambda q: Hh[:, Z.b, q, :], IDF[:], P).then_inc(ht_filled, 1)

        @block.scalar
        def _(act_engine):
            act = Queue(act_engine, RATES_ACT)
            ac = nc.scalar

            def exp_unit(it, k):
                n = it.ubase() + k
                g, i = divmod(k, 16 if it.full else 9)
                act.wait_ge(t_filled, n + 1)
                if it.full:
                    qd = k // 4
                    if i % 4 == 0:
                        act.wait_ge(pv_done, it.pbase() + (qd - 3 if qd >= 4 else (0 if it.b == 0 else qd - 3)))
                    dst = PT[:, 4 * (qd % 4) + k % 4, :]
                else:
                    if i == 0 and not (isinstance(it.t, int) and it.t == 0 and g < 2):
                        act.wait_ge(pv_done, it.pbase() + g - 1)
                    dst = PT[:, 9 * (g % 2) + i, :]
                ac.activation(dst, pT[:, k % 2, :], ACT.Exp, scale=SCALE).then_inc(t_used, 1)

            def copy_au(it, u):
                act.wait_ge(pv_done, it.pbase() + (8 if it.full else 2) * (u + 1))
                if not (isinstance(it.t, int) and it.t == 0):
                    act.wait_ge(num_filled, it.t)
                    act.wait_ge(den_filled, it.t)
                ac.copy(AU[:, u, :], pV[:, u, :]).then_inc(au_copied, 1)

            for b in range(NB):
                act.wait_ge(ht0_filled, b + 1)
                ac.copy(HT[:, b, :], pD[:, b % 2, :]).then_inc(ht0_copied, 1)

            for sl in slots(act):
                A, B, C, V, Z = sl.A, sl.B, sl.C, sl.V, sl.Dn
                for step in range(STEPS):
                    if C is not None:
                        for k in step_units(C, step):
                            exp_unit(C, k)
                    if step == 3 and Z is not None:
                        copy_au(Z, 1)
                    if step == 3 and C is not None and not C.full:
                        act.wait_ge(nm_done, C.t * 2 + 2)
                        if sl.s >= 1:
                            act.wait_ge(e_filled, C.t)
                        for u in range(2):
                            ins = ac.activation(EXM[:, :, HALF * u:HALF * (u + 1)], NM[:, u], ACT.Exp, scale=SCALE)
                        ins.then_inc(exm_done, 1)
                    if step == 6 and C is not None and not C.full:
                        act.wait_ge(e_filled, C.t + 1)
                        if sl.s >= 1:
                            act.wait_ge(e_out, C.t * 16)
                        ac.copy(ER[:], pD[0:H, 1, :]).then_inc(e_copied, 1)
                    if step in (12, 14) and A is not None:
                        x = 0 if step == 12 else 1
                        act.wait_ge(r1_done, A.t * 2 + 1 + x)
                        ac.copy(XS[:, x, 1, :], R1[:, x, :]).then_inc(mid_done, 1)
                    if step in (10, 12) and A is not None:
                        x = 0 if step == 10 else 1
                        act.wait_ge(qk_filled, A.t * 2 + 1 + x)
                        if sl.s >= -1:
                            act.wait_ge(parts_out, A.t * 96)
                        ac.activation(XS[:, x, 0, :], pD[:, 1 - x, :], ACT.Identity, bias=bqk[:, x:x + 1]) \
                            .then_inc(hi_done, 1)
                    if step == 21 and Z is not None:
                        act.wait_ge(h1t_filled, Z.t + 1)
                        if sl.s >= 2 or sl.reg is not None:
                            if Z.full and Z.b > 0:
                                act.wait_ge(ex_filled, 8 * Z.b)
                            else:
                                act.wait_ge(hid_filled, Z.t * 4)
                        ac.copy(H1T[:], pD[:, 1, :]).then_inc(h1t_copied, 1)
                    for j in GELUS[C is not None and C.full].get(step, ()):
                        if Z is not None and not Z.full:
                            if j == 0 and (sl.s >= 2 or sl.reg is not None):
                                act.wait_ge(y2_filled, Z.t)
                            act.wait_ge(hid_filled, Z.t * 4 + j + 1)
                            ac.activation(HIDT[:, j, :], pD[:, 1 - j % 2, :], ACT.Gelu, bias=b1[:, j:j + 1]) \
                                .then_inc(gelu_done, 1)
                    if step == 24 and Z is not None and Z.full:
                        act.wait_ge(lg_done, Z.t - NMASKED + 1)
                        ac.activation(PR[:], LG[:], ACT.Exp).then_inc(pe_done, 1)
                    if step == 28 and C is not None and not C.full:
                        copy_au(C, 0)
                    if step == 21 and C is not None and C.full:
                        copy_au(C, 0)
                    if step == STEPS - 1 and Z is not None and not Z.full:
                        act.wait_ge(ht_filled, Z.t + 1)
                        ac.copy(HT[:, Z.b, :], pD[:, 0, :]).then_inc(ht_copied, 1)

        @block.vector
        def _(dve_engine):
            dve = Queue(dve_engine, RATES_DVE)
            ve = nc.vector
            ch = Chain(dve, dve_step, DVE_STEPS)

            def max_unit(it, k):
                n = it.ubase() + k
                g, i = divmod(k, 16 if it.full else 9)
                tile, heads, blocks = unit_blocks(it.full, i)
                u, v = divmod(g, 2)
                dve.wait_ge(s_filled, n + 1)
                w = P * len(blocks)
                hs = 2 * heads[0] + v
                ve.tensor_reduce(MX[:, u, tile, hs:hs + 2 * len(heads) - 1:2],
                                 pS[:, k % 2, :].rearrange("p (h n) -> p h n", n=w),
                                 axis=AX.X, op=ALU.max).then_inc(s_used, 1)

            def neg_max(it, u):
                dve.wait_ge(s_used, it.ubase() + it.units() // 2 * (u + 1))
                if not (isinstance(it.t, int) and it.t == 0):
                    dve.wait_ge(mparts_done, it.t * 2 - 1 + u)
                    if not it.full:
                        dve.wait_ge(exm_done, it.t)
                    else:
                        dve.wait_ge(exm_done, NMASKED)
                if it.full:
                    ve.tensor_scalar(NM[:, u], MX[:, u], -1.0, None, ALU.mult).then_inc(nm_done, 1)
                else:
                    ve.scalar_tensor_tensor(out=NM[:, u], in0=MX[:, u], scalar=-1.0, in1=NFLOOR[:],
                                            op0=ALU.mult, op1=ALU.min).then_inc(nm_done, 1)

            def copy_shift(it, u):
                dve.wait_ge(m_filled, it.t * 2 + 1 + u)
                if not (isinstance(it.t, int) and it.t == 0):
                    dve.wait_ge(m_out, it.t * 32 - 16 + 16 * u)
                ve.tensor_copy(MROW[:, u, :], pD[0:3 * HALF, 0, :].bitcast(BF16)[:, 0:S]).then_inc(m_copied, 1)

            def stats(it, k):
                for q in range(QT):
                    ins = ve.bn_stats(BS[:, q, :], X[:, q, :])
                ch.link(ins)
                dve.eng.sem_inc(dve_passed, 1)
                for q in range(QT):
                    ins = ve.bn_aggr(MV[:, q, :], BS[:, q, :])
                ins.then_inc(ln_st, 1)

            def normalise(it, k):
                n = ln_no(it, k)
                dve.wait_ge(ln_rs, n + 1)
                for q in range(QT):
                    ins = ve.tensor_scalar(XN[:, q, :], X[:, q, :], NMEAN[:, q:q + 1], RS[:, q:q + 1],
                                           ALU.add, ALU.mult)
                return ins

            def rows(t):
                return t[:].unsqueeze(1).to_broadcast([P, QT, D])

            def times(gain):
                ch.link(ve.tensor_tensor(XN[:], XN[:], rows(gain), ALU.mult))

            def plus(bias, dst, *more):
                ins = ve.tensor_tensor(dst, XN[:], rows(bias), ALU.add)
                for m in more:
                    ch.link(ins)
                    ins = ve.tensor_tensor(dst, dst, m, ALU.add)
                return ins

            def gate(it):
                i = it.t - NMASKED
                dve.wait_ge(gate_filled, i + 1)
                ch.link(ve.tensor_tensor(LG[:], pD[:, 0, 0:QT * NE].rearrange("p (q e) -> p q e", e=NE),
                                         BG[:, :].unsqueeze(1).to_broadcast([P, QT, NE]), ALU.add))
                ch.link(ve.tensor_reduce(LM[:], LG[:], axis=AX.X, op=ALU.max))
                ve.tensor_tensor(LG[:], LG[:], LM[:, :].unsqueeze(2).to_broadcast([P, QT, NE]),
                                 ALU.subtract).then_inc(lg_done, 1)
                dve.wait_ge(pe_done, i + 1)
                ch.link(ve.tensor_reduce(LM[:], PR[:], axis=AX.X, op=ALU.add))
                ch.link(ve.reciprocal(LM[:], LM[:]))
                ch.link(ve.tensor_tensor(PR[:], PR[:], LM[:, :].unsqueeze(2).to_broadcast([P, QT, NE]), ALU.mult))
                pj = PR[:].unsqueeze(2).to_broadcast([P, QT, NE, NE])
                pe_ = PR[:].unsqueeze(3).to_broadcast([P, QT, NE, NE])
                ve.tensor_tensor(GT, pj, pe_, ALU.is_gt)
                ch.link(ve.tensor_tensor(EQ, pj, pe_, ALU.is_equal))
                ch.link(ve.tensor_tensor(EQ, EQ, TRI[:].unsqueeze(1).to_broadcast([P, QT, NE, NE]), ALU.mult))
                ch.link(ve.tensor_tensor(GT, GT, EQ, ALU.add))
                ch.link(ve.tensor_reduce(LG[:], GT, axis=AX.X, op=ALU.add))
                ch.link(ve.scalar_tensor_tensor(out=WT[:], in0=LG[:], scalar=2.0, in1=PR[:],
                                                op0=ALU.is_lt, op1=ALU.mult))

            def experts(it, i):
                q, e0 = divmod(i, 2)
                dve.wait_ge(ex_filled, (it.t - NMASKED) * 8 + i + 1)
                ve.tensor_tensor(YE, pD[:, i % 2, :], BEXP[:, e0 * S:(e0 + 1) * S], ALU.add).then_inc(ex_used, 1)
                dve.wait_ge(ex_used, (it.t - NMASKED) * 8 + i + 1)
                for e in range(4):
                    w = WT[:, q, 4 * e0 + e:4 * e0 + e + 1]
                    y = YE[:, e * P:(e + 1) * P]
                    if e0 == 0 and e == 0:
                        ch.link(ve.tensor_scalar(X[:, q, :], y, w, None, ALU.mult))
                    else:
                        ch.link(ve.scalar_tensor_tensor(out=X[:, q, :], in0=y, scalar=w, in1=X[:, q, :],
                                                        op0=ALU.mult, op1=ALU.add))

            ve.memset(Kop[:].rearrange("p a h n -> p (a h n)").bitcast(I32), 0).then_inc(setup_dve, 1)
            ve.memset(MHALF[:], -0.5).then_inc(setup_dve, 1)
            dve.wait_ge(pos_in, 32)
            for b in range(NB):
                dve.wait_ge(x_in, NB * 16)
                ve.tensor_tensor(Hh[:, b], Hh[:, b], XR[:], ALU.add).then_inc(posin, 1)
            dve.wait_ge(setup_pool, 5)

            for sl in slots(dve):
                ch.enter(sl)
                A, B, C, V, Z = sl.A, sl.B, sl.C, sl.V, sl.Dn
                if sl.s == -1 and sl.reg is None:
                    dve.wait_ge(consts_in, CONSTS * 16)
                if C is not None:
                    neg_max(C, 1)
                for step in range(STEPS):
                    if B is not None:
                        for k in step_units(B, step):
                            max_unit(B, k)
                    if step == 4 and C is not None:
                        copy_shift(C, 1)
                    if step == 7 and Z is not None:
                        dve.wait_ge(num_filled, Z.t + 1)
                        if sl.s >= 2 or sl.reg is not None:
                            dve.wait_ge(att_done, Z.t)
                        if not Z.full:
                            dve.wait_ge(tw_done, Z.t + 1)
                            ve.tensor_tensor(NUM[:], pD[:, 1, :], NUM[:], ALU.add).then_inc(num_done, 1)
                        else:
                            ve.tensor_copy(NUM[:], pD[:, 1, :]).then_inc(num_done, 1)
                    if step == 8 and Z is not None:
                        if not Z.full:
                            dve.wait_ge(den_filled, Z.t + 1)
                            dve.wait_ge(dn_done, Z.t + 1)
                            ve.tensor_tensor(DEN[:], pD[:, 0, :], DN[:], ALU.add).then_inc(den_done, 1)
                        else:
                            dve.wait_ge(den_filled, Z.t + 1)
                            ve.tensor_copy(DEN[:], pD[:, 0, :]).then_inc(den_done, 1)
                        dve.wait_ge(den_done, Z.t + 1)
                    if step in (8, 9, 10, 11) and Z is not None:
                        part = DEN[:, (step - 8) * P:(step - 7) * P]
                        ins = ve.reciprocal(part, part)
                        if step == 11:
                            ins.then_inc(rec_done, 1)
                    if step in (11, 13) and A is not None:
                        x = 0 if step == 11 else 1
                        dve.wait_ge(hi_done, A.t * 2 + 1 + x)
                        if sl.s >= -1:
                            dve.wait_ge(parts_done, A.t * 2 - 1 + x)
                        ve.scalar_tensor_tensor(out=R1[:, x, :], in0=pD[:, 1 - x, :], scalar=bqk[:, x:x + 1],
                                                in1=XS[:, x, 0, :], op0=ALU.add, op1=ALU.subtract) \
                            .then_inc(r1_done, 1)
                    if step == 15 and Z is not None:
                        dve.wait_ge(y_filled, Z.t + 1)
                        dve.wait_ge(hb_done, Z.t + 1)
                        ve.tensor_tensor(X[:].rearrange("p q n -> p (q n)"), pD[:, 1, :],
                                         HB[:].rearrange("p q n -> p (q n)"), ALU.add).then_inc(y_used, 1)
                        dve.wait_ge(y_used, Z.t + 1)
                        stats(Z, 0)
                    if step == 20 and C is not None and not C.full:
                        dve.wait_ge(wp_filled, C.t + 1)
                        dve.wait_ge(em_in, C.t * 16 + 16)
                        if sl.s >= 1:
                            dve.wait_ge(att_done, C.t)
                        ve.tensor_tensor(NUM[:], pD[:, 0, :], EM[:], ALU.mult).then_inc(tw_done, 1)
                    if step == 22:
                        if V is not None:
                            dve.wait_ge(v_filled, V.t + 1)
                            if sl.s >= 0:
                                dve.wait_ge(vp_done, V.t)
                                if C is not None and not C.full:
                                    dve.wait_ge(wp_filled, V.t)
                            ve.tensor_tensor(VC, pD[:, 0, :].rearrange("p (q n) -> p q n", q=QT),
                                             BV[:, :].unsqueeze(1).to_broadcast([P, QT, D]), ALU.add) \
                                .then_inc(v_done, 1)
                    if step == 17 and Z is not None:
                        ch.link(normalise(Z, 0))
                    if step == 18 and Z is not None:
                        times(G1)
                    if step == 19 and Z is not None:
                        if sl.s >= 2 or sl.reg is not None:
                            dve.wait_ge(h1t_filled, Z.t)
                            if not Z.full:
                                dve.wait_ge(h1b_done, Z.t)
                        if Z.full and Z.b > 0:
                            dve.wait_ge(out_done, 16 * Z.b)
                        plus(BE1, H1[:], *([Hh[:, Z.b]] if Z.full else [])).then_inc(h1_done, 1)
                    if step == 20 and B is not None:
                        neg_max(B, 0)
                    if step == 24 and Z is not None and Z.full:
                        gate(Z)
                    if step == 29 and B is not None:
                        copy_shift(B, 0)
                    if step in EX_STEPS and Z is not None and Z.full:
                        experts(Z, EX_STEPS.index(step))
                    if step == 35 and Z is not None and Z.full:
                        stats(Z, 1)
                    if step == 35 and Z is not None and Z.full:
                        normalise(Z, 1).then_inc(ln_xn, 1)
                        dve.wait_ge(z_done, Z.t - NMASKED + 1)
                        stats(Z, 2)
                        n = ln_no(Z, 2)
                        dve.wait_ge(ln_rs, n + 1)
                        for q in range(QT):
                            ins = ve.tensor_scalar(H1[:, q, :], X[:, q, :], NMEAN[:, q:q + 1], RS[:, q:q + 1],
                                                   ALU.add, ALU.mult)
                        ins.then_inc(out_ready, 1)
                    if step == 30 and Z is not None and not Z.full:
                        dve.wait_ge(y2_filled, Z.t + 1)
                        dve.wait_ge(h1b_done, Z.t + 1)
                        ve.tensor_tensor(X[:].rearrange("p q n -> p (q n)"), pD[:, 1, :],
                                         HB[:].rearrange("p q n -> p (q n)"), ALU.add).then_inc(y2_used, 1)
                        dve.wait_ge(y2_used, Z.t + 1)
                        stats(Z, 1)
                    if Z is not None and not Z.full and not Z.last:
                        if step == 32:
                            ch.link(normalise(Z, 1))
                        if step == 33:
                            times(G2)
                        if step == 34:
                            plus(BE2, Hh[:, Z.b]).then_inc(h2_done, 1)
                    if step == 33 and Z is not None and not Z.full:
                        if Z.last:
                            normalise(Z, 1).then_inc(ln_xn, 1)
                            dve.wait_ge(x2_done, Z.b + 1)
                            stats(Z, 2)
                            normalise(Z, 2).then_inc(ln_xn, 1)
                            dve.wait_ge(lnf_done, Z.b + 1)
                            stats(Z, 3)
                            dve.wait_ge(ln_rs, ln_no(Z, 3) + 1)
                            for q in range(QT):
                                ins = ve.tensor_scalar(Hh[:, Z.b, q, :], X[:, q, :], NMEAN[:, q:q + 1], RS[:, q:q + 1],
                                                       ALU.add, ALU.mult)
                            ins.then_inc(h2_done, 1)
            ch.enter(Slot(NITEMS + 1))

        @block.gpsimd
        def _(pool_engine):
            pool = Queue(pool_engine, RATES_POOL, pool_passed)
            gp = nc.gpsimd
            ch = Chain(pool, pool_step, POOL_STEPS)

            def split_max(it, u):
                pool.wait_ge(nm_done, it.t * 2 + 1 + u)
                if not (isinstance(it.t, int) and it.t == 0):
                    pool.wait_ge(m_filled, it.t * 2 - 1 + u)
                ch.link(gp.tensor_copy(SPL[:, u, :, 0, :], NM[:, u]))
                ch.link(gp.tensor_tensor(MR[:, u], NM[:, u], SPL[:, u, :, 0, :], ALU.subtract))
                ch.link(gp.tensor_copy(SPL[:, u, :, 1, :], MR[:, u]))
                gp.tensor_tensor(SPL[:, u, :, 2, :], MR[:, u], SPL[:, u, :, 1, :], ALU.subtract) \
                    .then_inc(mparts_done, 1)

            def parts(it, x):
                pool.wait_ge(mid_done, it.t * 2 + 1 + x)
                gp.tensor_tensor(XS[:, x, 2, :], R1[:, x, :], XS[:, x, 1, :], ALU.subtract).then_inc(parts_done, 1)

            def inverse_std(it, k):
                n = ln_no(it, k)
                pool.wait_ge(ln_st, n + 1)
                gp.tensor_scalar(NMEAN[:], MV[:, :, 0], -1.0, None, ALU.mult)
                ch.link(gp.tensor_scalar(VE[:], MV[:, :, 1], EPS, None, ALU.add))
                gp.tensor_tensor(RS[:], VE[:], MHALF[:], ALU.pow).then_inc(ln_rs, 1)

            def rows(t):
                return t[:].unsqueeze(1).to_broadcast([P, QT, D])

            def affine(it, k, gain, bias, dst, *more):
                pool.wait_ge(ln_xn, xn_no(it, k) + 1)
                ch.link(gp.tensor_tensor(dst, XN[:], rows(gain), ALU.mult))
                ins = gp.tensor_tensor(dst, dst, rows(bias), ALU.add)
                for m in more:
                    ch.link(ins)
                    ins = gp.tensor_tensor(dst, dst, m, ALU.add)
                return ins

            gp.memset(Qop[:].rearrange("p a h n -> p (a h n)").bitcast(F32), 0.0).then_inc(setup_pool, 1)
            gp.memset(ONES[:], 1.0)
            gp.memset(MX[:], 0.0).then_inc(setup_pool, 1)
            gp.memset(Vp[:], 0.0).then_inc(setup_pool, 1)
            pool.wait_ge(setup_pool, 3)
            for v in range(2):
                gp.memset(Vp[:, :, :, v:H:2, 16 * v + HD:16 * v + HD + 1]
                          .rearrange("p a q h o -> p (a q) (h o)"), 1.0).then_inc(setup_pool, 1)
            pool.wait_ge(setup_dve, 2)

            for sl in slots(pool):
                ch.enter(sl)
                if sl.s == -1 and sl.reg is None:
                    pool.wait_ge(consts_in, CONSTS * 16)
                A, B, C, V, Z = sl.A, sl.B, sl.C, sl.V, sl.Dn
                if C is not None:
                    split_max(C, 1)
                if Z is not None:
                    pool.wait_ge(wd_in, Z.l * 160 + 160)
                    if Z.full and Z.b > 0:
                        pool.wait_ge(y_used, Z.t)
                    elif sl.s >= 2 or sl.reg is not None:
                        pool.wait_ge(y2_used, Z.t)
                    if Z.full:
                        gp.tensor_copy(HB[:], rows(BO)).then_inc(hb_done, 1)
                    else:
                        gp.tensor_tensor(HB[:], Hh[:, Z.b], rows(BO), ALU.add).then_inc(hb_done, 1)
                    pool.wait_ge(rec_done, Z.t + 1)
                    if sl.s >= 2 or sl.reg is not None:
                        pool.wait_ge(y_filled, Z.t)
                    gp.tensor_tensor(ATT[:], NUM[:], DEN[:], ALU.mult).then_inc(att_done, 1)
                if A is not None:
                    parts(A, 0)
                if Z is not None:
                    inverse_std(Z, 0)
                if A is not None:
                    parts(A, 1)
                if Z is not None:
                    if not Z.full:
                        pool.wait_ge(h1_done, Z.t + 1)
                        gp.tensor_tensor(HB[:], H1[:], rows(B2), ALU.add).then_inc(h1b_done, 1)
                if C is not None and not C.full:
                    pool.wait_ge(em_in, C.t * 16 + 16)
                    if sl.s >= 1:
                        pool.wait_ge(den_done, C.t)
                    gp.tensor_tensor(DN[:], NMQ[:], EM[:], ALU.mult).then_inc(dn_done, 1)
                if B is not None:
                    split_max(B, 0)
                if V is not None:
                    pool.wait_ge(v_done, V.t + 1)
                    if sl.s >= 1:
                        pool.wait_ge(pv_done, Z.pbase() + (16 if Z.full else 4))
                    vc = VC.rearrange("p q (h v e) -> p (q h) v e", v=2, e=HD)
                    vp = Vp[:, V.par].rearrange("p q (h v) e -> p (q h) v e", v=2)
                    for v in range(2):
                        ins = gp.tensor_copy(vp[:, :, v, 16 * v:16 * v + HD], vc[:, :, v, :])
                    ins.then_inc(vp_done, 1)
                    if not V.full:
                        pair = [P, 2, D]
                        gp.tensor_tensor(VS[:, 4:6], VS[:, 1:3], VS[:, 3:4].to_broadcast(pair), ALU.add)
                        ch.link(gp.tensor_tensor(VS[:, 6:8], VS[:, 1:3], VS[:, 0:1].to_broadcast(pair), ALU.add))
                        gp.tensor_tensor(VS[:, 8:10], VS[:, 1:7:5], VS[:, 5:6].to_broadcast(pair), ALU.add) \
                            .then_inc(vs_done, 1)
                if Z is not None:
                    inverse_std(Z, 1)
                    if Z.full:
                        affine(Z, 1, G2, BE2, X[:], H1[:], Hh[:, Z.b]).then_inc(z_done, 1)
                        inverse_std(Z, 2)
                    elif Z.last:
                        affine(Z, 1, G2, BE2, X[:]).then_inc(x2_done, 1)
                        inverse_std(Z, 2)
                        pool.wait_ge(xr_in, Z.b * 16 + 16)
                        affine(Z, 2, GF, BF, X[:], XR[:]).then_inc(lnf_done, 1)
                        inverse_std(Z, 3)
            ch.enter(Slot(NITEMS + 1))


def constants():
    def bf(a):
        return (np.ascontiguousarray(a, np.float32).view(np.uint32) >> 16).astype(np.uint16)

    pos = np.arange(S)
    level = np.frexp((pos + 1).astype(np.float64))[1] - 1
    coord = (pos >> level) / 2.0 ** level
    div = np.exp(np.arange(0, D, 2, dtype=np.float64) * -(np.log(10000.0) / D))
    ang = pos[:, None].astype(np.float64) * div[None, :]
    pe = np.zeros((S, D), np.float32)
    pe[:, 0::2] = (np.sin(ang) * coord[:, None]).astype(np.float32)
    pe[:, 1::2] = (np.cos(ang) * coord[:, None]).astype(np.float32)
    masked = (pos[:, None] & pos[None, :]) != 0
    count = masked.sum(0).astype(np.float32)
    floor = np.where(count > 0, 0.0, 3e38).astype(np.float32).reshape(QT, P).T
    bits = ((pos[None, :] >> np.arange(9)[:, None]) & 1).astype(np.float32)
    sel = np.zeros((4, P, P), np.float32)
    for h in range(H):
        u, c, v = h // HALF, h % HALF // 2, h % 2
        for e in range(HD):
            sel[u, 32 * c + 16 * v + e, HD * h + e] = 1
            sel[2 + u, 32 * c + 16 * v + HD, HD * h + e] = 1
    tri = (np.arange(NE)[None, :] < np.arange(NE)[:, None]).astype(np.float32)
    return {
        "c_pos": pe,
        "c_idf": np.eye(P, dtype=np.float32),
        "c_idb": bf(np.eye(P)),
        "c_nfloor": np.ascontiguousarray(np.repeat(floor[:, :, None], HALF, 2).reshape(P, QT * HALF)),
        "c_krows": bf(np.concatenate([bits, np.ones((3, S), np.float32)])),
        "c_qrows": bf(-BIG * bits),
        "c_zero": bf(np.zeros((12, HALF * S))),
        "c_lowm": masked[0:P, 0:P].astype(np.float32),
        "c_nmq": count,
        "c_sel": sel.reshape(4 * P, P),
        "c_tri": np.ascontiguousarray(np.broadcast_to(tri.reshape(1, NE * NE), (P, NE * NE))),
    }


_INS = ["L0_attn_" + n for n in ("x", "Wq", "bq", "Wk", "bk", "Wv", "bv", "Wo", "bo", "W1", "b1", "W2", "b2",
                                 "ln1_g", "ln1_b", "ln2_g", "ln2_b", "lnf_g", "lnf_b")] + \
       ["L0_ffn_" + n for n in ("Wq", "bq", "Wk", "bk", "Wv", "bv", "Wo", "bo", "g1", "be1", "g2", "be2",
                                "Wg", "bg", "We", "bexp")]


def kernel(**inputs):
    import concourse.bacc as _bacc
    from concourse import mybir as _mybir
    from concourse.bass_utils import run_bass_kernel_spmd as _run

    nc = _bacc.Bacc("TRN2", target_bir_lowering=False, num_devices=1)
    arrays = {n: np.ascontiguousarray(inputs[n]) for n in _INS}
    arrays.update(constants())
    d = {n: nc.dram_tensor(n, a.shape, _mybir.dt.from_np(a.dtype), kind="ExternalInput").ap()
         for n, a in arrays.items()}
    for n in ("c_idb", "c_krows", "c_qrows", "c_zero"):
        d[n] = d[n].bitcast(BF16)
    out = nc.dram_tensor("out", (NB, S, D), F32, kind="ExternalOutput").ap()
    build(nc, d, out)
    r = _run(nc, [arrays], core_ids=[0])
    return r.results[0]["out"]
```
